# Optimizing a Trainium2 kernel written in Bass

```python
import numpy as np
import jax
import jax.numpy as jnp

def _softmax(x, axis=-1):
    return jax.nn.softmax(x, axis=axis)

def _gelu(x):
    return jax.nn.gelu(x, approximate=True)

def _silu(x):
    return jax.nn.silu(x)

def _sigmoid(x):
    return jax.nn.sigmoid(x)

def _layernorm(x, axis=-1, eps=1e-05):
    m = jnp.mean(x, axis=axis, keepdims=True)
    v = jnp.var(x, axis=axis, keepdims=True)
    return (x - m) / jnp.sqrt(v + eps)

def _scatter_add(tgt, idx, src, axis=0):
    return tgt.at[idx].add(src)

def _segment_sum(src, seg, n):
    return jax.ops.segment_sum(src, seg, n)
kernel_name = 'mk_sandwich_d1_jaxref_r8_37dac5'

def setup_inputs(seed: int=0):
    np.random.seed(seed)
    _w = jnp.asarray

    def _L0_attn_setup():
        import jax, jax.numpy as jnp
        import numpy as np
        B, N, DIM = (2, 256, 128)
        HEADS, DHEAD = (16, 64)
        GNN_DEPTH = 2
        EPS = 1e-05

        def layer_norm(x, gamma):
            mu = jnp.mean(x, axis=-1, keepdims=True)
            var = jnp.var(x, axis=-1, keepdims=True)
            return (x - mu) / jnp.sqrt(var + EPS) * gamma
        key = jax.random.key(seed)
        ks = jax.random.split(key, 12)
        hd = HEADS * DHEAD
        s = lambda fan: 1.0 / np.sqrt(fan)
        return {'x': jax.random.normal(ks[0], (B, N, DIM), dtype=jnp.float32), 'gamma_in': jnp.ones((DIM,), dtype=jnp.float32), 'Wq': jax.random.normal(ks[1], (DIM, hd), dtype=jnp.float32) * s(DIM), 'Wk': jax.random.normal(ks[2], (DIM, hd), dtype=jnp.float32) * s(DIM), 'Wv': jax.random.normal(ks[3], (DIM, hd), dtype=jnp.float32) * s(DIM), 'gnn_w': jax.random.normal(ks[4], (GNN_DEPTH, DHEAD, DHEAD), dtype=jnp.float32) * s(DHEAD), 'gnn_b': jnp.zeros((GNN_DEPTH, DHEAD), dtype=jnp.float32), 'lin_w': jax.random.normal(ks[5], (DHEAD, DHEAD), dtype=jnp.float32) * s(DHEAD), 'lin_b': jnp.zeros((DHEAD,), dtype=jnp.float32), 'Wo': jax.random.normal(ks[6], (hd, DIM), dtype=jnp.float32) * s(hd), 'gamma_out': jnp.ones((DIM,), dtype=jnp.float32)}
    _L0_attn_in = _L0_attn_setup()

    def _L0_ffn_setup():
        import jax, jax.numpy as jnp
        import numpy as np
        DIM = 128
        DEPTH = 2
        HEADS = 8
        DIM_HEAD = 64
        WINDOW = 64
        INNER = HEADS * DIM_HEAD
        HID = int(DIM * 4 * 2 / 3)
        B, N = (2, 1024)
        QK_SCALE = 8.0

        def shift_token(t):
            t1, t2 = jnp.split(t, 2, axis=-1)
            t2 = jnp.pad(t2, ((0, 0), (1, 0), (0, 0)))[:, :-1]
            return jnp.concatenate([t1, t2], axis=-1)

        def l2norm(t):
            return t / jnp.clip(jnp.linalg.norm(t, axis=-1, keepdims=True), 1e-12)

        def rotate_half(x):
            x1, x2 = jnp.split(x, 2, axis=-1)
            return jnp.concatenate([-x2, x1], axis=-1)

        def rotary_xpos(q, k):
            n = q.shape[-2]
            half_idx = jnp.arange(0, DIM_HEAD, 2, dtype=jnp.float32)
            inv_freq = 1.0 / 10000.0 ** (half_idx / DIM_HEAD)
            t = jnp.arange(n, dtype=jnp.float32)
            freqs = t[:, None] * inv_freq[None, :]
            freqs = jnp.concatenate([freqs, freqs], axis=-1)
            base = (half_idx + 0.4 * DIM_HEAD) / (1.4 * DIM_HEAD)
            power = (t - n // 2) / float(WINDOW // 2)
            scale = base[None, :] ** power[:, None]
            scale = jnp.concatenate([scale, scale], axis=-1)
            cos, sin = (jnp.cos(freqs), jnp.sin(freqs))
            q = q * cos * scale + rotate_half(q) * sin * scale
            k = k * cos / scale + rotate_half(k) * sin / scale
            return (q, k)

        def local_attention(q, k, v):
            b, h, n, d = q.shape
            w = n // WINDOW
            bq = q.reshape(b, h, w, WINDOW, d) * QK_SCALE
            bk = k.reshape(b, h, w, WINDOW, d)
            bv = v.reshape(b, h, w, WINDOW, d)

            def look_around(t):
                p = jnp.pad(t, ((0, 0), (0, 0), (1, 0), (0, 0), (0, 0)))
                return jnp.concatenate([p[:, :, :w], p[:, :, 1:]], axis=3)
            bk, bv = (look_around(bk), look_around(bv))
            bt = jnp.arange(n).reshape(w, WINDOW)
            btp = jnp.pad(bt, ((1, 0), (0, 0)), constant_values=-1)
            btk = jnp.concatenate([btp[:w], btp[1:]], axis=1)
            sim = jnp.einsum('bhwid,bhwjd->bhwij', bq, bk)
            i = bt[:, :, None]
            j = btk[:, None, :]
            mask = (i < j) | (i > j + WINDOW) | (j == -1)
            sim = jnp.where(mask, -jnp.finfo(sim.dtype).max, sim)
            attn = jax.nn.softmax(sim, axis=-1)
            out = jnp.einsum('bhwij,bhwjd->bhwid', attn, bv)
            return out.reshape(b, h, n, d)

        def _layer(x, wqkv, qs, ksc, wo, lg, lb, w1, b1, w2, b2):
            b, n, _ = x.shape
            h = shift_token(x)
            qkv = h @ wqkv
            q, k, v = jnp.split(qkv, 3, axis=-1)
            to_heads = lambda t: t.reshape(b, n, HEADS, DIM_HEAD).transpose(0, 2, 1, 3)
            q, k, v = (to_heads(q), to_heads(k), to_heads(v))
            q = l2norm(q) * qs
            k = l2norm(k) * ksc
            q, k = rotary_xpos(q, k)
            o = local_attention(q, k, v)
            o = o.transpose(0, 2, 1, 3).reshape(b, n, INNER)
            x = x + o @ wo
            h = shift_token(x)
            mu = h.mean(-1, keepdims=True)
            var = h.var(-1, keepdims=True)
            h = (h - mu) / jnp.sqrt(var + 1e-05) * lg + lb
            h = h @ w1 + b1
            a, g = jnp.split(h, 2, axis=-1)
            h = a * jax.nn.gelu(g, approximate=False)
            x = x + h @ w2 + b2
            return x
        key = jax.random.key(seed)
        ks = jax.random.split(key, 6)
        return {'x': jax.random.normal(ks[0], (B, N, DIM), jnp.float32), 'wqkv': jax.random.normal(ks[1], (DEPTH, DIM, 3 * INNER), jnp.float32) * 0.02, 'q_scale': jnp.ones((DEPTH, DIM_HEAD), jnp.float32), 'k_scale': jnp.ones((DEPTH, DIM_HEAD), jnp.float32), 'wo': jax.random.normal(ks[2], (DEPTH, INNER, DIM), jnp.float32) * 0.02, 'ln_g': jnp.ones((DEPTH, DIM), jnp.float32), 'ln_b': jnp.zeros((DEPTH, DIM), jnp.float32), 'w1': jax.random.normal(ks[3], (DEPTH, DIM, 2 * HID), jnp.float32) * 0.02, 'b1': jnp.zeros((DEPTH, 2 * HID), jnp.float32), 'w2': jax.random.normal(ks[4], (DEPTH, HID, DIM), jnp.float32) * 0.02, 'b2': jnp.zeros((DEPTH, DIM), jnp.float32)}
    _L0_ffn_in = _L0_ffn_setup()
    _d = {'L0_attn_x': _L0_attn_in['x'], 'L0_attn_gamma_in': _L0_attn_in['gamma_in'], 'L0_attn_Wq': _L0_attn_in['Wq'], 'L0_attn_Wk': _L0_attn_in['Wk'], 'L0_attn_Wv': _L0_attn_in['Wv'], 'L0_attn_gnn_w': _L0_attn_in['gnn_w'], 'L0_attn_gnn_b': _L0_attn_in['gnn_b'], 'L0_attn_lin_w': _L0_attn_in['lin_w'], 'L0_attn_lin_b': _L0_attn_in['lin_b'], 'L0_attn_Wo': _L0_attn_in['Wo'], 'L0_attn_gamma_out': _L0_attn_in['gamma_out'], 'L0_ffn_wqkv': _L0_ffn_in['wqkv'], 'L0_ffn_q_scale': _L0_ffn_in['q_scale'], 'L0_ffn_k_scale': _L0_ffn_in['k_scale'], 'L0_ffn_wo': _L0_ffn_in['wo'], 'L0_ffn_ln_g': _L0_ffn_in['ln_g'], 'L0_ffn_ln_b': _L0_ffn_in['ln_b'], 'L0_ffn_w1': _L0_ffn_in['w1'], 'L0_ffn_b1': _L0_ffn_in['b1'], 'L0_ffn_w2': _L0_ffn_in['w2'], 'L0_ffn_b2': _L0_ffn_in['b2']}
    _x0 = _d['L0_attn_x']
    _d['L0_attn_x'] = jax.random.normal(jax.random.fold_in(jax.random.key(seed), 1), (2, 1024, 128), dtype=_x0.dtype)
    del _x0
    return _d

def reference(L0_attn_x, L0_attn_gamma_in, L0_attn_Wq, L0_attn_Wk, L0_attn_Wv, L0_attn_gnn_w, L0_attn_gnn_b, L0_attn_lin_w, L0_attn_lin_b, L0_attn_Wo, L0_attn_gamma_out, L0_ffn_wqkv, L0_ffn_q_scale, L0_ffn_k_scale, L0_ffn_wo, L0_ffn_ln_g, L0_ffn_ln_b, L0_ffn_w1, L0_ffn_b1, L0_ffn_w2, L0_ffn_b2):

    def _L0_attn_ref(x, gamma_in, Wq, Wk, Wv, gnn_w, gnn_b, lin_w, lin_b, Wo, gamma_out):
        import jax, jax.numpy as jnp
        import numpy as np
        B, N, DIM = (2, 256, 128)
        HEADS, DHEAD = (16, 64)
        GNN_DEPTH = 2
        EPS = 1e-05

        def layer_norm(x, gamma):
            mu = jnp.mean(x, axis=-1, keepdims=True)
            var = jnp.var(x, axis=-1, keepdims=True)
            return (x - mu) / jnp.sqrt(var + EPS) * gamma
        b, n, _ = x.shape
        scale = DHEAD ** (-0.5)
        xn = layer_norm(x, gamma_in)
        q = (xn @ Wq).reshape(b, n, HEADS, DHEAD).transpose(0, 2, 1, 3) * scale
        k = (xn @ Wk).reshape(b, n, HEADS, DHEAD).transpose(0, 2, 1, 3)
        v = (xn @ Wv).reshape(b, n, HEADS, DHEAD).transpose(0, 2, 1, 3)
        sim = jnp.einsum('bhid,bhjd->bhij', q, k)
        mask_value = -jnp.finfo(sim.dtype).max
        causal_mask = jnp.triu(jnp.ones((n, n), dtype=bool), k=1)
        sim = jnp.where(causal_mask, mask_value, sim)
        attn = jax.nn.softmax(sim.astype(jnp.float32), axis=-1)
        out = jnp.einsum('bhij,bhjd->bhid', attn, v)
        adj = attn.reshape(b * HEADS, n, n)
        adj = jnp.clip(adj + jnp.eye(n, dtype=adj.dtype), 0.0, 1.0)
        deg = jnp.sum(adj, axis=-1, keepdims=True)
        feats = v.reshape(b * HEADS, n, DHEAD)
        for l in range(GNN_DEPTH):
            h = feats @ gnn_w[l] + gnn_b[l]
            h = jnp.einsum('bij,bjd->bid', adj, h) / deg
            feats = jax.nn.gelu(h + feats, approximate=False)
        gnn_out = feats @ lin_w + lin_b
        out = out + gnn_out.reshape(b, HEADS, n, DHEAD)
        out = out.transpose(0, 2, 1, 3).reshape(b, n, HEADS * DHEAD)
        return layer_norm(out @ Wo, gamma_out)

    def _L0_ffn_ref(x, wqkv, q_scale, k_scale, wo, ln_g, ln_b, w1, b1, w2, b2):
        import jax, jax.numpy as jnp
        import numpy as np
        DIM = 128
        DEPTH = 2
        HEADS = 8
        DIM_HEAD = 64
        WINDOW = 64
        INNER = HEADS * DIM_HEAD
        HID = int(DIM * 4 * 2 / 3)
        B, N = (2, 1024)
        QK_SCALE = 8.0

        def shift_token(t):
            t1, t2 = jnp.split(t, 2, axis=-1)
            t2 = jnp.pad(t2, ((0, 0), (1, 0), (0, 0)))[:, :-1]
            return jnp.concatenate([t1, t2], axis=-1)

        def l2norm(t):
            return t / jnp.clip(jnp.linalg.norm(t, axis=-1, keepdims=True), 1e-12)

        def rotate_half(x):
            x1, x2 = jnp.split(x, 2, axis=-1)
            return jnp.concatenate([-x2, x1], axis=-1)

        def rotary_xpos(q, k):
            n = q.shape[-2]
            half_idx = jnp.arange(0, DIM_HEAD, 2, dtype=jnp.float32)
            inv_freq = 1.0 / 10000.0 ** (half_idx / DIM_HEAD)
            t = jnp.arange(n, dtype=jnp.float32)
            freqs = t[:, None] * inv_freq[None, :]
            freqs = jnp.concatenate([freqs, freqs], axis=-1)
            base = (half_idx + 0.4 * DIM_HEAD) / (1.4 * DIM_HEAD)
            power = (t - n // 2) / float(WINDOW // 2)
            scale = base[None, :] ** power[:, None]
            scale = jnp.concatenate([scale, scale], axis=-1)
            cos, sin = (jnp.cos(freqs), jnp.sin(freqs))
            q = q * cos * scale + rotate_half(q) * sin * scale
            k = k * cos / scale + rotate_half(k) * sin / scale
            return (q, k)

        def local_attention(q, k, v):
            b, h, n, d = q.shape
            w = n // WINDOW
            bq = q.reshape(b, h, w, WINDOW, d) * QK_SCALE
            bk = k.reshape(b, h, w, WINDOW, d)
            bv = v.reshape(b, h, w, WINDOW, d)

            def look_around(t):
                p = jnp.pad(t, ((0, 0), (0, 0), (1, 0), (0, 0), (0, 0)))
                return jnp.concatenate([p[:, :, :w], p[:, :, 1:]], axis=3)
            bk, bv = (look_around(bk), look_around(bv))
            bt = jnp.arange(n).reshape(w, WINDOW)
            btp = jnp.pad(bt, ((1, 0), (0, 0)), constant_values=-1)
            btk = jnp.concatenate([btp[:w], btp[1:]], axis=1)
            sim = jnp.einsum('bhwid,bhwjd->bhwij', bq, bk)
            i = bt[:, :, None]
            j = btk[:, None, :]
            mask = (i < j) | (i > j + WINDOW) | (j == -1)
            sim = jnp.where(mask, -jnp.finfo(sim.dtype).max, sim)
            attn = jax.nn.softmax(sim, axis=-1)
            out = jnp.einsum('bhwij,bhwjd->bhwid', attn, bv)
            return out.reshape(b, h, n, d)

        def _layer(x, wqkv, qs, ksc, wo, lg, lb, w1, b1, w2, b2):
            b, n, _ = x.shape
            h = shift_token(x)
            qkv = h @ wqkv
            q, k, v = jnp.split(qkv, 3, axis=-1)
            to_heads = lambda t: t.reshape(b, n, HEADS, DIM_HEAD).transpose(0, 2, 1, 3)
            q, k, v = (to_heads(q), to_heads(k), to_heads(v))
            q = l2norm(q) * qs
            k = l2norm(k) * ksc
            q, k = rotary_xpos(q, k)
            o = local_attention(q, k, v)
            o = o.transpose(0, 2, 1, 3).reshape(b, n, INNER)
            x = x + o @ wo
            h = shift_token(x)
            mu = h.mean(-1, keepdims=True)
            var = h.var(-1, keepdims=True)
            h = (h - mu) / jnp.sqrt(var + 1e-05) * lg + lb
            h = h @ w1 + b1
            a, g = jnp.split(h, 2, axis=-1)
            h = a * jax.nn.gelu(g, approximate=False)
            x = x + h @ w2 + b2
            return x
        for l in range(DEPTH):
            x = _layer(x, wqkv[l], q_scale[l], k_scale[l], wo[l], ln_g[l], ln_b[l], w1[l], b1[l], w2[l], b2[l])
        return x
    x = L0_attn_x
    x = x + _layernorm(_L0_attn_ref(_layernorm(x, axis=-1), L0_attn_gamma_in, L0_attn_Wq, L0_attn_Wk, L0_attn_Wv, L0_attn_gnn_w, L0_attn_gnn_b, L0_attn_lin_w, L0_attn_lin_b, L0_attn_Wo, L0_attn_gamma_out), axis=-1)
    x = x + _layernorm(_L0_ffn_ref(_layernorm(x, axis=-1), L0_ffn_wqkv, L0_ffn_q_scale, L0_ffn_k_scale, L0_ffn_wo, L0_ffn_ln_g, L0_ffn_ln_b, L0_ffn_w1, L0_ffn_b1, L0_ffn_w2, L0_ffn_b2), axis=-1)
    return x

_drawn_inputs = setup_inputs


def setup_inputs(seed=0):
    import zlib

    import numpy as np

    out = dict(_drawn_inputs(seed))
    spreads = {'L0_attn_gamma_in': (1.0, 0.2),
     'L0_attn_gnn_b': (0.0, 0.1),
     'L0_attn_lin_b': (0.0, 0.1),
     'L0_attn_gamma_out': (1.0, 0.2),
     'L0_ffn_q_scale': (1.0, 0.6),
     'L0_ffn_k_scale': (1.0, 0.6),
     'L0_ffn_ln_g': (1.0, 0.6),
     'L0_ffn_ln_b': (0.0, 0.8),
     'L0_ffn_b1': (0.0, 0.8),
     'L0_ffn_b2': (0.0, 0.8)}
    factors = {'L0_ffn_w1': 7.285, 'L0_ffn_w2': 7.26}
    for name, (base, spread) in spreads.items():
        noise = np.random.default_rng([zlib.crc32(name.encode()), seed]).standard_normal(out[name].shape)
        drawn = base * np.exp(spread * noise) if base else spread * noise
        out[name] = jnp.asarray(drawn.astype(out[name].dtype))
    for name, factor in factors.items():
        out[name] = (out[name] * factor).astype(out[name].dtype)
    return out
```

```python
from contextlib import ExitStack

import numpy as np

import concourse.bass as bass
from concourse import mybir

F32 = mybir.dt.float32
F32R = mybir.dt.float32r
BF16 = mybir.dt.bfloat16
ACT = mybir.ActivationFunctionType
ALU = mybir.AluOpType
AX = mybir.AxisListType

P = 128
NB, NT, DM = 2, 1024, 128
NBLK = NT // P
HA, DH = 16, 64
HB = 8
INNER = HB * DH
HID = 341
DEPTH = 2
EPS = 1e-5
BIG = float(2.0 ** 100)


class Eng:

    def __init__(self, sem):
        self.sem, self.n, self.ops, self.seen = sem, 0, [], {}

    def need(self, *marks):
        for m in marks:
            if m is not None and self.seen.get(id(m[0]), 0) < m[1]:
                self.seen[id(m[0])] = m[1]
                self.ops.append((m[0], m[1]))

    def do(self, fn, sig=True):
        if sig:
            self.n += 1
        self.ops.append((fn, sig))
        return (self.sem, self.n) if sig else None

    def dma(self, fn, sem, count):
        self.ops.append((fn, sem, count))

    def emit(self, eng):
        for op in self.ops:
            if len(op) == 3:
                op[0](eng).then_inc(op[1], 16)
            elif callable(op[0]):
                ins = op[0](eng)
                if op[1]:
                    ins.then_inc(self.sem, 1)
            else:
                eng.wait_ge(op[0], op[1])


def program(nc, I, OUT):
    with ExitStack() as ctx:
        cnt = [0]
        scope = [ctx]

        def sb(shape, dt=F32):
            cnt[0] += 1
            return scope[0].enter_context(nc.sbuf_tensor(f"t{cnt[0]}", shape, dt))

        def ar(n):
            return sb([P, n])[:, :]

        def sem(name):
            return ctx.enter_context(nc.semaphore(name))

        pe, dve, act, pool, sp = (Eng(sem("s_" + n)) for n in ("pe", "dve", "act", "pool", "sp"))
        PS = ctx.enter_context(nc.psum_tensor("PS", [P, 8 * 512], F32))
        bank_free = [[] for _ in range(8)]

        def bank(k, n=1):
            return PS[:, k * 512:(k + n) * 512]

        def own(k, n=1):
            for b in range(k, k + n):
                pe.need(*bank_free[b])

        def free(k, *marks):
            bank_free[k] = list(marks)

        nload = [0]

        def load(dst, src, after=()):
            s = sem(f"ld{nload[0]}")
            nload[0] += 1
            sp.need(*after)
            sp.dma(lambda e: e.dma_start(dst, src), s, 16)
            return (s, 16)

        x0 = sb([P, 16, DM])
        x_tiles = I["L0_attn_x"].rearrange("b (k p) d -> p (b k) d", p=P)
        m_x = load(x0[:], x_tiles)
        identF = sb([P, P])
        gam_in = sb([P, DM])
        cm = sb([P, 2, P])
        m_id = load(identF[:], I["c_ident"])
        m_gin = load(gam_in[:], I["L0_attn_gamma_in"].rearrange("(a d) -> a d", a=1).broadcast_to([P, DM]))
        m_cm = load(cm[:], I["c_causal"].rearrange("a p d -> p a d"))
        identR = sb([P, P], F32R)
        identB = sb([P, P], BF16)
        half = sb([P, 16])
        fsc = sb([P, 2])
        st6 = sb([P, 16, 6])
        mv = sb([P, 16, 2])
        rs = sb([P, 16])
        first = ExitStack()
        scope[0] = first
        WqD = ar(1024).rearrange("p (h d) -> p h d", h=HA)
        WkD = ar(1024).rearrange("p (h d) -> p h d", h=HA)
        m_wq = [load(WqD, I["L0_attn_Wq"].rearrange("f (h d) -> f h d", h=HA))]
        m_wk = [load(WkD, I["L0_attn_Wk"].rearrange("f (h d) -> f h d", h=HA))]
        WV2 = ar(2048).rearrange("p (h d) -> p h d", h=HA)
        OF = [ar(1024).rearrange("p (k d) -> p k d", k=8) for _ in range(2)]
        Wv = OF[0].rearrange("p k d -> p (k d)")
        m_wv = load(Wv[:], I["L0_attn_Wv"])
        m_wv2 = load(WV2[:, :, 0:DH], I["L0_attn_Wv"].rearrange("f (h d) -> f h d", h=HA))
        WO = ar(2048).rearrange("p (h d) -> p h d", h=HA)
        m_wo = load(WO[0:DH, :, :], I["L0_attn_Wo"].rearrange("(h e) n -> e h n", h=HA))
        w0d = sb([P, P])
        m_z0 = dve.do(lambda e: e.memset(w0d[:], 0.0))
        m_w0d = [load(w0d[t * DH:(t + 1) * DH, t * DH:(t + 1) * DH], I["L0_attn_gnn_w"][0], after=[m_z0]) for t in range(2)]
        WG = sb([DH, P])
        m_wg = [load(WG[:, 0:DH], I["c_ident"][0:DH, 0:DH]), load(WG[:, DH:P], I["L0_attn_gnn_w"][0])]
        WW1 = sb([P, DH])
        m_ww1 = [load(WW1[t * DH:(t + 1) * DH, :], I["L0_attn_gnn_w"][1]) for t in range(2)]
        linw = sb([DH, DH])
        m_lw = load(linw[:], I["L0_attn_lin_w"])
        linb = sb([DH, 1])
        m_lb = load(linb[:], I["L0_attn_lin_b"].rearrange("(d a) -> d a", a=1))
        gb = sb([P, 2, DH])
        m_gb = [load(gb[:, t, :], I["L0_attn_gnn_b"][t:t + 1, :].broadcast_to([P, DH])) for t in range(2)]
        gam_out = sb([P, DM])
        m_gout = load(gam_out[:], I["L0_attn_gamma_out"].rearrange("(a d) -> a d", a=1).broadcast_to([P, DM]))

        cmB = sb([P, 2, P], BF16)
        dve.need(m_id, m_cm)
        m_idR = dve.do(lambda e: e.tensor_copy(identR[:], identF[:]))
        dve.do(lambda e: e.tensor_copy(identB[:], identF[:]))
        m_cmB = dve.do(lambda e: e.tensor_copy(cmB[:], cm[:]))
        m_half = pool.do(lambda e: e.memset(half[:], -0.5))

        def layernorm(dst, src, m_src, ks=range(16), gam=None, m_gam=None, bet=None):
            ks = list(ks)
            a, z = ks[0], ks[-1] + 1
            for k in ks:
                dve.need(m_src(k))
                m = dve.do(lambda e, k=k: e.bn_stats(st6[:, k, :], src[:, k, :]))
            dve.need(m)
            for k in ks:
                m = dve.do(lambda e, k=k: e.bn_aggr(mv[:, k, :], st6[:, k, :]))
            dve.need(m)
            m = dve.do(lambda e: e.tensor_scalar(rs[:, a:z], mv[:, a:z, 1], EPS, None, ALU.add))
            pool.need(m, m_half)
            m = pool.do(lambda e: e.tensor_tensor(rs[:, a:z], rs[:, a:z], half[:, a:z], ALU.pow))
            dve.need(m, m_gam)
            out = {}
            for k in ks:
                out[k] = dve.do(lambda e, k=k: e.tensor_scalar(dst[:, k, :], src[:, k, :], mv[:, k, 0:1], rs[:, k:k + 1],
                                                               ALU.subtract, ALU.mult))
            for t, op in ((gam, ALU.mult), (bet, ALU.add)):
                if t is not None:
                    dve.need(out[ks[-1]])
                    m = dve.do(lambda e, t=t, op=op: e.tensor_tensor(dst[:, a:z, :], dst[:, a:z, :],
                                                                    t[:].unsqueeze(1).broadcast_to([P, z - a, DM]), op))
                    out = {k: m for k in ks}
            return out

        xn = ar(2048).rearrange("p (k d) -> p k d", k=16)
        xnT = ar(2048)
        m = layernorm(xn, x0, lambda k: m_x)
        m = layernorm(xn, xn, lambda k: m[15], gam=gam_in, m_gam=m_gin)
        for g in range(4):
            own(g)
            pe.need(m[15], m_id)
            for r in range(4):
                t = pe.do(lambda e, g=g, r=r: e.transpose(bank(g)[:, r * P:(r + 1) * P], xn[:, 4 * g + r, :], identF[:]), r == 3)
            act.need(t)
            m_xnT = act.do(lambda e, g=g: e.copy(xnT[:, g * 512:(g + 1) * 512], bank(g)))
            free(g, m_xnT)

        WvT = xn.rearrange("p k d -> p (k d)")
        for g in range(2):
            own(4 + g)
            pe.need(m_wv, m_xnT)
            for r in range(4):
                t = pe.do(lambda e, g=g, r=r: e.transpose(bank(4 + g)[:, r * P:(r + 1) * P],
                                                          Wv[:, (4 * g + r) * P:(4 * g + r + 1) * P], identF[:]), r == 3)
            act.need(t)
            m_wvT = act.do(lambda e, g=g: e.copy(WvT[:, g * 512:(g + 1) * 512], bank(4 + g)))
            free(4 + g, m_wvT)
        pe.need(m_wvT, *m_w0d)
        for g in range(2):
            own(6 + g)
            for r in range(4):
                t = pe.do(lambda e, g=g, r=r: e.matmul(bank(6 + g)[:, r * P:(r + 1) * P],
                                                       WvT[:, (4 * g + r) * P:(4 * g + r + 1) * P], w0d[:],
                                                       start=True, stop=True), r == 3)
            act.need(t)
            m_wv2p = act.do(lambda e, g=g: e.copy(WV2[:, 8 * g:8 * g + 8, DH:P],
                                                  bank(6 + g).rearrange("p (h d) -> p h d", h=8)))
            free(6 + g, m_wv2p)
        LW = sb([DH, P])
        LBc = sb([DH, P])
        m_lz = dve.do(lambda e: e.memset(LW[:], 0.0))
        own(0)
        pe.need(m_lw)
        t = pe.do(lambda e: e.transpose(bank(0)[0:DH, 0:DH], linw[:], identF[0:DH, 0:DH]))
        dve.need(t, m_lb, m_lz)
        m_LW = dve.do(lambda e: e.tensor_copy(LW[:, DH:P], bank(0)[0:DH, 0:DH]))
        m_LBc = dve.do(lambda e: e.tensor_copy(LBc[:], linb[:].broadcast_to([DH, P])))
        free(0, m_LW)
        pe.need(m_LW, m_LBc, m_wo)
        for g in range(4):
            own(g)
            t = pe.do(lambda e, g=g: e.matmul(bank(g), LW[:], WO[0:DH, 4 * g:4 * g + 4, :], start=True, stop=True))
            act.need(t)
            m_WO = act.do(lambda e, g=g: e.copy(WO[DH:P, 4 * g:4 * g + 4, :],
                                                bank(g)[DH:P].rearrange("p (h d) -> p h d", h=4)))
            free(g, m_WO)
        own(4)
        for h in range(HA):
            t = pe.do(lambda e, h=h: e.matmul(bank(4)[:, 0:P], LBc[:], WO[0:DH, h, :], start=(h == 0), stop=(h == HA - 1)),
                      h == HA - 1)
        ylin = sb([P, P])
        dve.need(t)
        m_ylin = dve.do(lambda e: e.tensor_copy(ylin[:], bank(4)[:, 0:P]))
        free(4, m_ylin)

        R3 = 2
        Q1 = [sb([P, NT], F32R) for _ in range(R3)]
        K1 = [sb([P, NT], F32R) for _ in range(R3)]
        K2 = [sb([66, NT], F32R) for _ in range(R3)]
        Q2 = [sb([66, NT], F32R) for _ in range(R3)]
        vF = [ar(512).rearrange("p (k d) -> p k d", k=8) for _ in range(R3)]
        vB = [ar(512).rearrange("p (k d) -> p k d", k=8) for _ in range(R3)]
        vW = [ar(512).rearrange("p (k d) -> p k d", k=8) for _ in range(R3)]
        VH = [sb([P, 8, 66], F32R) for _ in range(R3)]
        VL = [sb([P, 8, 66], F32R) for _ in range(R3)]
        WD = [sb([P, 2, 2, DH]) for _ in range(2)]
        NM = [sb([P, 8, 66], F32R) for _ in range(2)]
        nm = [sb([P, 8]) for _ in range(2)]
        EC = 4608
        Eh = sb([P, EC], F32R)
        El = sb([P, EC], F32R)
        NS = 3
        Es = ar(NS * 512).rearrange("p (s n) -> p s n", s=NS)
        dscr = ar(128)
        eD = [sb([P, 8]) for _ in range(2)]
        RT = sb([66, NT])
        RT2 = ar(NT)
        gZ = [sb([P, 4, 8]) for _ in range(2)]
        t1 = ar(512).rearrange("p (k d) -> p k d", k=8)
        t2 = ar(512).rearrange("p (k d) -> p k d", k=8)
        fF = [ar(512).rearrange("p (k d) -> p k d", k=8) for _ in range(2)]
        fB = ar(512).rearrange("p (k d) -> p k d", k=8)
        gf = ar(512).rearrange("p (k d) -> p k d", k=8)
        F2 = sb([P, 8, P], F32R)
        G2 = sb([P, 8, P], F32R)
        OFT = ar(1024)
        Y = xn
        ini = sb([P, 2, 66])
        m_i0 = dve.do(lambda e: e.memset(ini[:, 0, :], 0.0))
        m_i1 = dve.do(lambda e: e.memset(ini[:, 1, :], 1.0))
        dve.need(m_i0, m_i1)
        ini_m = []
        for i in range(R3):
            ini_m.append(dve.do(lambda e, i=i: e.tensor_copy(VL[i][:, :, 64:66], ini[:, 0:1, 0:2].broadcast_to([P, 8, 2]))))
            ini_m.append(dve.do(lambda e, i=i: e.tensor_copy(VH[i][:, :, 64:66], ini[:, 1:2, 0:2].broadcast_to([P, 8, 2]))))
            ini_m.append(dve.do(lambda e, i=i: e.tensor_copy(K2[i][64:66, :], ini[64:66, 1, 0:1].broadcast_to([2, NT]))))
        for i in range(2):
            ini_m.append(dve.do(lambda e, i=i: e.tensor_copy(NM[i][:, :, 0:64], ini[:, 0:1, 0:64].broadcast_to([P, 8, 64]))))
        m_ini = ini_m[-1]
        dve.need(m_ylin, m_wv2p)
        for b in range(NB):
            m_Y = dve.do(lambda e, b=b: e.tensor_copy(Y[:, 8 * b:8 * b + 8, :], ylin[:].unsqueeze(1).broadcast_to([P, 8, P])))

        tiles = []
        off = 0
        for c in range(2):
            for jb in range(4 * c + 4):
                i0 = max(c * 512, jb * P)
                n = (c + 1) * 512 - i0
                tiles.append((c, jb, i0, n, off))
                off += n
        assert off == EC
        NH = NB * HA
        S = [dict() for _ in range(NH)]

        def f32(ap):
            return ap.bitcast(F32)

        def old(t, key):
            return S[t][key] if t >= 0 else None

        def proj(t):
            b, h = divmod(t, HA)
            r, s = t % R3, S[t]
            pool.need(*m_wq, *m_wk, old(t - 2, "proj"))
            for i, W in enumerate((WkD, WqD)):
                md = pool.do(lambda e, i=i, W=W: e.tensor_copy(WD[r][:, i, :, :], W[:, h:h + 1, :].broadcast_to([P, 2, DH])))
            pe.need(m_xnT, m_WO, m_wv2p, m_wv2, md)
            for i, (which, T1) in enumerate((("k", K1[r]), ("q", Q1[r]))):
                sc = 0.125 if which == "q" else 1.0
                for c in range(2):
                    bk = 6 + c
                    sl = slice(c * 512, (c + 1) * 512)
                    own(bk)
                    mm = pe.do(lambda e, i=i, bk=bk, c=c: e.matmul(bank(bk), WD[r][:, i, :, :].rearrange("p t d -> p (t d)"),
                                                                   xnT[:, b * NT + c * 512:b * NT + (c + 1) * 512],
                                                                   start=True, stop=True))
                    s["proj"] = mm
                    act.need(mm, old(t - R3, "av"), old(t - R3, "smax_pe"), m_ini)
                    mh = act.do(lambda e, T1=T1, sl=sl, bk=bk, sc=sc: e.activation(T1[:, sl], bank(bk), ACT.Copy, scale=sc))
                    dve.need(mm, mh, old(t - R3, "av"))
                    if which == "k":
                        ml = dve.do(lambda e, T1=T1, sl=sl, bk=bk: e.tensor_tensor(K2[r][0:64, sl], bank(bk)[0:64, :],
                                                                                   f32(T1[0:64, sl]), ALU.subtract))
                        free(bk, mh, ml)
                        s["kl"] = ml
                    else:
                        m2 = act.do(lambda e, sl=sl, bk=bk: e.activation(Q2[r][0:64, sl], bank(bk)[0:64, :], ACT.Copy, scale=0.125))
                        ml = dve.do(lambda e, T1=T1, sl=sl, bk=bk: e.scalar_tensor_tensor(
                            T1[64:128, sl], bank(bk)[64:128, :], 0.125, f32(T1[64:128, sl]), ALU.mult, ALU.subtract))
                        free(bk, m2, ml)
                        s["q2"] = m2
                        s["ql"] = ml
            for c in range(2):
                bk = 6 + c
                own(bk)
                for k in range(4):
                    mm = pe.do(lambda e, bk=bk, c=c, k=k: e.matmul(bank(bk)[:, k * P:(k + 1) * P],
                                                                   xnT[:, b * NT + (4 * c + k) * P:b * NT + (4 * c + k + 1) * P],
                                                                   WV2[:, h, :], start=True, stop=True), k == 3)
                pv = bank(bk).rearrange("p (k d) -> p k d", k=4)
                ks = slice(4 * c, 4 * c + 4)
                act.need(mm, old(t - R3, "n6"), old(t - R3, "av"))
                a1 = act.do(lambda e, pv=pv, ks=ks: e.copy(vF[r][:, ks, :], pv[:, :, 0:DH]))
                a2 = act.do(lambda e, pv=pv, ks=ks: e.copy(vW[r][:, ks, :], pv[:, :, DH:P]))
                a3 = act.do(lambda e, pv=pv, ks=ks: e.copy(VH[r][:, ks, 0:DH], pv[:, :, 0:DH]))
                dve.need(a3)
                d1 = dve.do(lambda e, pv=pv, ks=ks: e.tensor_tensor(VL[r][:, ks, 0:DH], pv[:, :, 0:DH],
                                                                    f32(VH[r][:, ks, 0:DH]), ALU.subtract))
                free(bk, a3, d1)
                s["va"], s["vl"] = a3, d1
            pool.need(a1, *m_gb)
            s["vb"] = pool.do(lambda e: e.tensor_tensor(vB[r][:, :, :], vF[r][:, :, :],
                                                        gb[:, 0:1, :].broadcast_to([P, 8, DH]), ALU.add))

        def smax(t):
            r, s = t % R3, S[t]
            pe.need(s["ql"], s["kl"], s["q2"], m_cmB)
            for ib in range(8):
                w = (ib + 1) * P
                b0 = 0 if ib >= 4 else ib % 2
                nb = 2 if ib >= 4 else 1
                own(b0, nb)
                for c in range(nb):
                    lo, hi = c * 512, min(w, (c + 1) * 512)
                    pe.do(lambda e, b0=b0, c=c, lo=lo, hi=hi, ib=ib, last=(hi == w): e.matmul(
                        bank(b0 + c)[:, 0:hi - lo], Q1[r][:, ib * P:(ib + 1) * P], K1[r][:, lo:hi],
                        start=True, stop=not last), False)
                d0 = (ib * P) % 512
                mm = pe.do(lambda e, bb=b0 + nb - 1, d0=d0: e.matmul(bank(bb)[:, d0:d0 + P], identB[:], cmB[:, 0, :],
                                                                     start=False, stop=True))
                dve.need(mm, old(t - 2, "mrow_pe"))
                md = dve.do(lambda e, b0=b0, nb=nb, w=w, ib=ib: e.tensor_reduce(
                    nm[t % 2][:, ib:ib + 1], bank(b0, nb)[:, 0:w], AX.X, ALU.max, negate=True))
                for k in range(nb):
                    free(b0 + k, md)
            s["smax_pe"] = mm
            dve.need(md)
            m1 = dve.do(lambda e: e.tensor_copy(NM[t % 2][:, :, 64], nm[t % 2][:]))
            dve.need(m1)
            s["nm"] = dve.do(lambda e: e.tensor_tensor(NM[t % 2][:, :, 65], nm[t % 2][:], f32(NM[t % 2][:, :, 64]), ALU.subtract))

        def mrow(t):
            r, s = t % R3, S[t]
            pe.need(s["nm"], m_idR)
            for c in range(2):
                own(6 + c)
                for k in range(4):
                    mm = pe.do(lambda e, c=c, k=k: e.matmul(bank(6 + c)[0:66, k * P:(k + 1) * P], NM[t % 2][:, 4 * c + k, :],
                                                            identR[:], start=True, stop=True), k == 3)
                act.need(mm)
                s["q2m"] = act.do(lambda e, c=c: e.copy(Q2[r][64:66, c * 512:(c + 1) * 512], bank(6 + c)[64:66, :]))
                free(6 + c, s["q2m"])
            s["mrow_pe"] = mm

        est = [None] * NS
        enum = [0]

        def scores(t, fill):
            r, u, s = t % R3, t % 2, S[t]
            pe.need(s["q2m"], s["kl"], s["ql"], s["vl"], s["va"])
            ready = {}
            LAG = 3

            def av(k):
                c, jb, i0, n, o = tiles[k]
                if jb == 0:
                    own(4)
                pe.need(ready[k])
                dst = bank(4)[0:66, i0 - c * 512:512]
                pe.do(lambda e: e.matmul(dst, VH[r][:, jb, :], Eh[:, o:o + n], start=(jb == 0), stop=False), False)
                pe.do(lambda e: e.matmul(dst, VL[r][:, jb, :], Eh[:, o:o + n], start=False, stop=False), False)
                mm = pe.do(lambda e: e.matmul(dst, VH[r][:, jb, :], El[:, o:o + n], start=False, stop=(jb == 4 * c + 3)))
                if jb == 4 * c + 3:
                    act.need(mm, old(t - 1, "g0"))
                    s["rt"] = act.do(lambda e: e.copy(RT[:, c * 512:(c + 1) * 512], bank(4)[0:66, :]))
                    free(4, s["rt"])
                s["av"] = mm

            for k, (c, jb, i0, n, o) in enumerate(tiles):
                bk = 2 + k % 2
                own(bk)
                diag = jb >= 4 * c
                mm = pe.do(lambda e, bk=bk, jb=jb, i0=i0, n=n: e.matmul(bank(bk)[:, 0:n], K1[r][:, jb * P:(jb + 1) * P],
                                                                        Q1[r][:, i0:i0 + n], start=True, stop=False), False)
                mm = pe.do(lambda e, bk=bk, jb=jb, i0=i0, n=n, d=diag: e.matmul(
                    bank(bk)[:, 0:n], K2[r][:, jb * P:(jb + 1) * P], Q2[r][:, i0:i0 + n], start=False, stop=not d), not diag)
                if diag:
                    mm = pe.do(lambda e, bk=bk: e.matmul(bank(bk)[:, 0:P], identB[:], cmB[:, 1, :], start=False, stop=True))
                q = enum[0] % NS
                enum[0] += 1
                act.need(mm, est[q])
                me = act.do(lambda e, bk=bk, n=n, q=q: e.activation(Es[:, q, 0:n], bank(bk)[:, 0:n], ACT.Exp))
                free(bk, me)
                dve.need(me, old(t - 1, "l2"))
                mh = dve.do(lambda e, n=n, q=q, o=o: e.tensor_copy(Eh[:, o:o + n], Es[:, q, 0:n]))
                if diag:
                    dve.need(old(t - 2, "gz"), s.get("e") or old(t - 1, "e"))
                    s["e"] = dve.do(lambda e, q=q, jb=jb: e.scalar_tensor_tensor(
                        dscr[:, 0:P], Es[:, q, 0:P], 1.0, identF[:], ALU.mult, ALU.mult, accum_out=eD[u][:, jb:jb + 1]))
                dve.need(mh)
                ready[k] = dve.do(lambda e, n=n, q=q, o=o: e.tensor_tensor(El[:, o:o + n], Es[:, q, 0:n],
                                                                           f32(Eh[:, o:o + n]), ALU.subtract))
                est[q] = ready[k]
                if k >= LAG:
                    av(k - LAG)
            fill()
            for k in range(len(tiles) - LAG, len(tiles)):
                av(k)

        def bc(ap):
            return ap.unsqueeze(2).broadcast_to([P, 8, DH])

        def graph1(t):
            r, u, s = t % R3, t % 2, S[t]
            pe.need(s["rt"], *m_wg)
            own(4)
            for k in range(8):
                mz = pe.do(lambda e, k=k: e.matmul(bank(4)[:, k:k + 1], RT[64:66, k * P:(k + 1) * P], identF[64:66, 64:65],
                                                   start=True, stop=True), k == 7)
            gm = []
            for c in range(2):
                own(6 + c)
                for k in range(4):
                    mm = pe.do(lambda e, c=c, k=k: e.matmul(bank(6 + c)[:, k * P:(k + 1) * P],
                                                            RT[0:64, (4 * c + k) * P:(4 * c + k + 1) * P], WG[:],
                                                            start=True, stop=True), k == 3)
                gm.append(mm)
            s["g0"] = mm
            g = gZ[u]
            dve.need(mz, s["e"], old(t - 2, "p1"))
            a = dve.do(lambda e: e.tensor_copy(g[:, 0, :], bank(4)[:, 0:8]))
            free(4, a)
            dve.need(a)
            a = dve.do(lambda e: e.tensor_tensor(g[:, 1, :], g[:, 0, :], eD[u][:], ALU.subtract))
            dve.need(a)
            b_ = dve.do(lambda e: e.tensor_tensor(g[:, 3, :], g[:, 0, :], g[:, 1, :], ALU.add))
            c_ = dve.do(lambda e: e.reciprocal(g[:, 2, :], g[:, 0, :]))
            dve.need(b_)
            d_ = dve.do(lambda e: e.reciprocal(g[:, 3, :], g[:, 3, :]))
            s["gz"] = d_
            pool.need(a, s["va"], old(t - 1, "n3"))
            n2 = pool.do(lambda e: e.tensor_tensor(t1, vW[r], bc(g[:, 1, :]), ALU.mult))
            dve.need(n2, d_, c_, *gm)
            dve.need(old(t - 2, "ofT"))
            for c in range(2):
                ks = slice(4 * c, 4 * c + 4)
                pv = bank(6 + c).rearrange("p (k d) -> p k d", k=4)
                n1 = dve.do(lambda e, ks=ks, pv=pv: e.tensor_tensor(OF[t % 2][:, ks, 0:DH], pv[:, :, 0:DH],
                                                                    bc(g[:, 2, :])[:, ks, :], ALU.mult))
                n3 = dve.do(lambda e, ks=ks, pv=pv: e.tensor_tensor(t1[:, ks, :], t1[:, ks, :], pv[:, :, DH:P], ALU.add))
                free(6 + c, n3)
            s["o1"] = n1
            dve.need(n3)
            n4 = dve.do(lambda e: e.tensor_tensor(t1, t1, bc(g[:, 3, :]), ALU.mult))
            dve.need(n4, s["vb"], old(t - 1, "ge1"))
            n6 = dve.do(lambda e: e.tensor_tensor(t2, t1, vB[r], ALU.add))
            s["n3"] = s["n6"] = n6
            act.need(n6, old(t - 2, "fuse"))
            s["ge1"] = act.do(lambda e: e.activation(fF[u], t2, ACT.Gelu))
            act.need(s["ge1"], old(t - 1, "l2"))
            a = act.do(lambda e: e.copy(F2[:, :, 0:DH], fF[u]))
            pool.need(s["ge1"], old(t - 1, "gl"))
            p = pool.do(lambda e: e.tensor_tensor(gf, fF[u], bc(g[:, 1, :]), ALU.mult))
            dve.need(a, old(t - 1, "l2"))
            d1 = dve.do(lambda e: e.tensor_tensor(F2[:, :, DH:P], fF[u], f32(F2[:, :, 0:DH]), ALU.subtract))
            act.need(p)
            a2 = act.do(lambda e: e.copy(G2[:, :, 0:DH], gf))
            dve.need(a2, p)
            s["gl"] = dve.do(lambda e: e.tensor_tensor(G2[:, :, DH:P], gf, f32(G2[:, :, 0:DH]), ALU.subtract))
            s["f2"] = [a, d1, a2, s["gl"]]

        def graph2(t):
            u, s = t % 2, S[t]
            pe.need(*s["f2"])
            for c in range(2):
                own(5)
                for (cc, jb, i0, n, o) in tiles:
                    if cc != c:
                        continue
                    dst = bank(5)[:, i0 - c * 512:512]
                    pe.do(lambda e, d=dst, jb=jb, n=n, o=o: e.matmul(d, F2[:, jb, :], Eh[:, o:o + n],
                                                                     start=(jb == 0), stop=False), False)
                    pe.do(lambda e, d=dst, jb=jb, n=n, o=o: e.matmul(d, F2[:, jb, :], El[:, o:o + n],
                                                                     start=False, stop=False), False)
                for k in range(4):
                    mm = pe.do(lambda e, k=k, c=c: e.matmul(bank(5)[:, k * P:(k + 1) * P], G2[:, 4 * c + k, :], identR[:],
                                                            start=False, stop=(k == 3)), k == 3)
                act.need(mm, old(t - 1, "r2w"))
                s["rt2"] = act.do(lambda e, c=c: e.copy(RT2[:, c * 512:(c + 1) * 512], bank(5)))
                free(5, s["rt2"])
            s["l2"] = mm

        def graph2b(t):
            u, s = t % 2, S[t]
            own(5)
            pe.need(s["rt2"], *m_ww1)
            for k in range(8):
                mm = pe.do(lambda e, k=k: e.matmul(bank(5)[:, k * DH:(k + 1) * DH], RT2[:, k * P:(k + 1) * P], WW1[:],
                                                   start=True, stop=True), k == 7)
            s["r2w"] = mm
            pool.need(s["ge1"], old(t - 1, "p2"))
            fb = pool.do(lambda e: e.tensor_tensor(fB, fF[u], gb[:, 1:2, :].broadcast_to([P, 8, DH]), ALU.add))
            s["fuse"] = fb
            dve.need(mm, fb)
            p1 = dve.do(lambda e: e.tensor_tensor(t3, bank(5).rearrange("p (k d) -> p k d", k=8), bc(gZ[u][:, 3, :]), ALU.mult))
            free(5, p1)
            s["p1"] = p1
            dve.need(p1, old(t - 1, "ge2"))
            s["p2"] = dve.do(lambda e: e.tensor_tensor(t4, t3, fB, ALU.add))
            act.need(s["p2"], s["o1"])
            s["ge2"] = act.do(lambda e: e.activation(OF[t % 2][:, :, DH:P], t4, ACT.Gelu))

        def tail(t):
            b, h = divmod(t, HA)
            s = S[t]
            pe.need(s["ge2"], s["o1"])
            for c in range(2):
                own(6 + c)
                for k in range(4):
                    mm = pe.do(lambda e, c=c, k=k: e.transpose(bank(6 + c)[:, k * P:(k + 1) * P], OF[t % 2][:, 4 * c + k, :],
                                                               identF[:]), k == 3)
                act.need(mm, old(t - 1, "y"))
                a = act.do(lambda e, c=c: e.copy(OFT[:, c * 512:(c + 1) * 512], bank(6 + c)))
                free(6 + c, a)
            s["ofT"] = mm
            pe.need(a)
            for c in range(2):
                own(6 + c)
                for k in range(4):
                    mm = pe.do(lambda e, c=c, k=k: e.matmul(bank(6 + c)[:, k * P:(k + 1) * P],
                                                            OFT[:, (4 * c + k) * P:(4 * c + k + 1) * P], WO[:, h, :],
                                                            start=True, stop=True), k == 3)
                dve.need(mm, m_Y if t == 0 else S[t - 1]["yd"])
                ks = slice(8 * b + 4 * c, 8 * b + 4 * c + 4)
                d = dve.do(lambda e, c=c, ks=ks: e.tensor_tensor(Y[:, ks, :], Y[:, ks, :],
                                                                 bank(6 + c).rearrange("p (k d) -> p k d", k=4), ALU.add))
                free(6 + c, d)
            s["y"], s["yd"] = mm, d

        t3 = ar(512).rearrange("p (k d) -> p k d", k=8)
        t4 = ar(512).rearrange("p (k d) -> p k d", k=8)
        proj(0)
        smax(0)
        mrow(0)
        for t in range(NH + 2):
            if t + 1 < NH:
                proj(t + 1)
                smax(t + 1)
            if 0 <= t - 1 < NH:
                graph2(t - 1)

            def fill():
                if 0 <= t - 1 < NH:
                    graph2b(t - 1)
                if t + 1 < NH:
                    mrow(t + 1)
            if t < NH:
                scores(t, fill)
            else:
                fill()
            if 0 <= t - 2 < NH:
                tail(t - 2)
            if t < NH:
                graph1(t)

        m_y = S[NH - 1]["yd"]
        m = layernorm(Y, Y, lambda k: m_y, gam=gam_out, m_gam=m_gout)
        mm_ = m[15]
        m = layernorm(Y, Y, lambda k: mm_)
        dve.need(m[15])
        m_x1 = dve.do(lambda e: e.tensor_tensor(x0[:], x0[:], Y, ALU.add))

        own(7)
        fence = (pe.do(lambda e: e.transpose(bank(7)[:, 0:P], identF[:], identF[:])), m_x1,
                 act.do(lambda e: e.copy(fsc[:, 0:1], identF[:, 0:1])), pool.do(lambda e: e.memset(fsc[:, 1:2], 0.0)))
        free(7, fence[0])
        for q in (pe, dve, act, pool, sp):
            q.need(*fence)
        first.close()
        scope[0] = ctx
        X = ar(2048).rearrange("p (k d) -> p k d", k=16)
        ffn(nc, I, ctx, locals())
        block = ctx.enter_context(nc.Block())
        block.sync(lambda e: sp.emit(e))
        block.tensor(lambda e: pe.emit(e))
        block.vector(lambda e: dve.emit(e))
        block.scalar(lambda e: act.emit(e))
        block.gpsimd(lambda e: pool.emit(e))


def ffn(nc, I, ctx, g):
    pe, dve, act, pool, sp = (g[n] for n in ("pe", "dve", "act", "pool", "sp"))
    X, x0, ar, load, bank, own, free, sb, layernorm = (g[n] for n in (
        "X", "x0", "ar", "load", "bank", "own", "free", "sb", "layernorm"))
    identF, identB, sem, half, fence, OUT = (g[n] for n in ("identF", "identB", "sem", "half", "fence", "OUT"))
    F = list(fence)

    wqkv = ar(1536)
    wo = ar(512).rearrange("p (c n) -> p c n", c=4)
    w1 = ar(2 * HID)
    w2 = ar(384).rearrange("p (c n) -> p c n", c=3)
    tab = ar(4 * 512).rearrange("p (s k d) -> p s k d", s=4, k=8)
    tabl = ar(4 * 512).rearrange("p (s k d) -> p s k d", s=4, k=8)
    qks = ar(4 * DH).rearrange("p (s d) -> p s d", s=4)
    lgb = ar(3 * DM).rearrange("p (s d) -> p s d", s=3)
    b1 = ar(2 * HID)
    H = ar(2048).rearrange("p (k d) -> p k d", k=16)
    HT = ar(2048)
    qk = [ar(1024) for _ in range(2)]
    qr = ar(1024)
    tm = ar(1024)
    sq = ar(1024)
    ss = [ar(16) for _ in range(2)]
    KT = ar(4 * 1024).rearrange("p (c n) -> p c n", c=4)
    QT = ar(512).rearrange("p (c n) -> p c n", c=4)
    V = ar(8 * 512).rearrange("p (k n) -> p k n", k=8)
    E = ar(8 * 256).rearrange("p (h n) -> p h n", h=8)
    ET = ar(8 * 256).rearrange("p (h n) -> p h n", h=8)
    nmx = ar(8)
    Z = ar(8)
    rZ = ar(8)
    O = ar(512)
    OT = ar(512)
    A = ar(HID)
    G = ar(HID)
    PT = ar(384).rearrange("p (c n) -> p c n", c=3)
    bandF = ar(256)
    band = sb([P, 256], BF16)
    m_band = load(bandF, I["c_band"])
    dve.need(m_band)
    m_bandB = dve.do(lambda e: e.tensor_copy(band[:], bandF))
    m_tab = load(tab, I["c_rot"].rearrange("s (k p) d -> p s k d", p=P))
    m_h0 = dve.do(lambda e: e.memset(H[:, :, :], 0.0))

    m = layernorm(X, x0, lambda k: None)
    m_X = m[15]
    m_res = None
    last_h = m_h0
    rel = F
    s_sh = sem("shift")
    nsh = [0]

    def shifted(m_src, m_free):
        sp.need(m_src, *m_free)
        for b in range(NB):
            k0 = 8 * b
            sp.dma(lambda e, k0=k0: e.dma_start(H[1:P, k0:k0 + 8, 64:128], X[0:P - 1, k0:k0 + 8, 64:128]), s_sh, 16)
            sp.dma(lambda e, k0=k0: e.dma_start(H[0:1, k0 + 1:k0 + 8, 64:128], X[P - 1:P, k0:k0 + 7, 64:128]), s_sh, 16)
            nsh[0] += 2
        dve.need(m_src, *m_free)
        d = dve.do(lambda e: e.tensor_copy(H[:, :, 0:64], X[:, :, 0:64]))
        return [d, (s_sh, 16 * nsh[0])]

    def transposed(m_src, m_free):
        pe.need(*m_src)
        for q in range(4):
            own(q)
            for r in range(4):
                t = pe.do(lambda e, q=q, r=r: e.transpose(bank(q)[:, r * P:(r + 1) * P], H[:, 4 * q + r, :], identF[:]), r == 3)
            act.need(t, *m_free)
            a = act.do(lambda e, q=q: e.copy(HT[:, q * 512:(q + 1) * 512], bank(q)))
            free(q, a)
        return t, a

    hfree = [m_h0]
    htfree = []
    for l in range(DEPTH):
        m_w = [load(wqkv, I["L0_ffn_wqkv"][l], after=rel), load(wo, I["L0_ffn_wo"][l].rearrange("(c p) n -> p c n", p=P)),
               load(w1, I["L0_ffn_w1"][l]),
               load(w2[:, 0:2, :], I["L0_ffn_w2"][l][0:256, :].rearrange("(c p) n -> p c n", p=P)),
               load(w2[0:85, 2, :], I["L0_ffn_w2"][l][256:HID, :]),
               load(lgb[:, 0, :], I["L0_ffn_ln_g"][l:l + 1, :].broadcast_to([P, DM])),
               load(lgb[:, 1, :], I["L0_ffn_ln_b"][l:l + 1, :].broadcast_to([P, DM])),
               load(lgb[:, 2, :], I["L0_ffn_b2"][l:l + 1, :].broadcast_to([P, DM])),
               load(b1, I["L0_ffn_b1"][l:l + 1, :].broadcast_to([P, 2 * HID]))]
        for s, name in enumerate(("L0_ffn_q_scale", "L0_ffn_k_scale")):
            src = I[name][l:l + 1, :]
            m_w += [load(qks[:, 2 * s, :], src.broadcast_to([P, DH])),
                    load(qks[:, 2 * s + 1, 0:32], src[:, 32:64].broadcast_to([P, 32])),
                    load(qks[:, 2 * s + 1, 32:64], src[:, 0:32].broadcast_to([P, 32]))]
        pool.need(m_tab, *m_w)
        for s in range(4):
            m_tl = pool.do(lambda e, s=s: e.tensor_tensor(tabl[:, s, :, :], tab[:, s, :, :],
                                                          qks[:, s:s + 1, :].broadcast_to([P, 8, DH]), ALU.mult))
        mh = shifted(m_X, hfree)
        t_h, m_HT = transposed(mh, htfree)
        hfree = [t_h]
        prev = dict()
        for k in range(16):
            kb, b = k % 8, k // 8
            pe.need(m_HT, *m_w)
            mq = []
            for c in range(3):
                own(c)
                mq.append(pe.do(lambda e, c=c, k=k: e.matmul(bank(c), HT[:, k * P:(k + 1) * P], wqkv[:, c * 512:(c + 1) * 512],
                                                             start=True, stop=True)))
            act.need(mq[2], prev.get("av1"), prev.get("av"))
            a_v = act.do(lambda e, kb=kb: e.copy(V[:, kb, :], bank(2)))
            free(2, a_v)
            act.need(mq[1], prev.get("ss"))
            a_s = act.do(lambda e: e.activation(sq, bank(0, 2), ACT.Square))
            dve.need(a_s)
            u = k % 2
            d = dve.do(lambda e, u=u: e.tensor_reduce(ss[u], sq.rearrange("p (s d) -> p s d", d=DH), AX.X, ALU.add))
            dve.need(d)
            prev["ss"] = d
            d = dve.do(lambda e, u=u: e.tensor_scalar(ss[u], ss[u], 1e-24, None, ALU.max))
            pool.need(d)
            p = pool.do(lambda e, u=u: e.tensor_tensor(ss[u], ss[u], half[:], ALU.pow))
            dve.need(p, prev.get("sum"))
            d = dve.do(lambda e, u=u: e.tensor_tensor(qk[0].rearrange("p (s d) -> p s d", d=DH),
                                                      bank(0, 2).rearrange("p (s d) -> p s d", d=DH),
                                                      ss[u].unsqueeze(2).broadcast_to([P, 16, DH]), ALU.mult))
            free(0, d)
            free(1, d)
            m_qn = d
            dve.need(d, m_tl)
            pool.need(d)
            q4 = qk[0].rearrange("p (s h d) -> p s h d", s=2, d=DH)
            t4 = tm.rearrange("p (s h d) -> p s h d", s=2, d=DH)
            r4 = qr.rearrange("p (s h d) -> p s h d", s=2, d=DH)
            dve.need(prev.get("tq"))
            for s in range(2):
                ds = dve.do(lambda e, s=s, kb=kb: e.tensor_tensor(r4[:, s, :, :], q4[:, s, :, :],
                                                                  tabl[:, 2 * s, kb:kb + 1, :].broadcast_to([P, 8, DH]), ALU.mult))
                for hf in range(2):
                    dt = dve.do(lambda e, s=s, kb=kb, hf=hf: e.tensor_tensor(
                        t4[:, s, :, 32 * hf:32 * hf + 32], q4[:, s, :, 32 - 32 * hf:64 - 32 * hf],
                        tabl[:, 2 * s + 1, kb:kb + 1, 32 * hf:32 * hf + 32].broadcast_to([P, 8, 32]), ALU.mult))
            dve.need(dt, ds)
            d = dve.do(lambda e: e.tensor_tensor(qr, qr, tm, ALU.add))
            prev["sum"] = d
            pe.need(d)
            for s in range(2):
                own(3 + s)
                for c in range(4):
                    t = pe.do(lambda e, s=s, c=c: e.transpose(bank(3 + s)[:, c * P:(c + 1) * P],
                                                              qr[:, s * 512 + c * P:s * 512 + (c + 1) * P], identF[:]), c == 3)
                act.need(t, prev.get("s_pe"))
                dstT = QT if s == 0 else KT[:, :, kb * P:(kb + 1) * P]
                a = act.do(lambda e, s=s, dstT=dstT: e.copy(dstT, bank(3 + s).rearrange("p (c n) -> p c n", c=4)))
                free(3 + s, a)
            prev["tq"] = t
            pe.need(a, m_bandB)
            lo = 0 if kb else P
            own(4, 4)
            for hp in range(4):
                for j in range(2):
                    bk, o = 4 + 2 * j + hp // 2, 256 * (hp % 2)
                    rows = slice(64 * j, 64 * j + 64)
                    t = pe.do(lambda e, bk=bk, o=o, rows=rows, hp=hp, kb=kb, lo=lo: e.matmul(
                        bank(bk)[:, o + lo:o + 256], QT[rows, hp, :], KT[rows, hp, kb * P - P + lo:kb * P + P],
                        start=True, stop=False), False)
                    t = pe.do(lambda e, bk=bk, o=o, lo=lo: e.matmul(bank(bk)[:, o + lo:o + 256], identB[:],
                                                                    band[:, lo:256], start=False, stop=True))
            prev["s_pe"] = t
            sv = bank(4, 4).rearrange("p (h n) -> p h n", h=8)
            dve.need(t, prev.get("exp"))
            d = dve.do(lambda e, lo=lo: e.tensor_reduce(nmx, sv[:, :, lo:256], AX.X, ALU.max, negate=True))
            dve.need(d)
            d = dve.do(lambda e: e.tensor_scalar(nmx, nmx, 8.0, None, ALU.mult))
            act.need(d, prev.get("te"), prev.get("rz"))
            for at in range(8):
                h = 2 * (at % 4) + at // 4
                a = act.do(lambda e, h=h, at=at, lo=lo: e.activation(E[:, h, lo:256], sv[:, at, lo:256], ACT.Exp,
                                                                     bias=nmx[:, at:at + 1], scale=8.0, accum_out=Z[:, h:h + 1]))
                if at % 2:
                    free(4 + at // 2, a)
            prev["exp"] = a
            dve.need(a)
            rz = dve.do(lambda e: e.reciprocal(rZ, Z))
            prev["rz"] = rz
            pe.need(a)
            nc_ = 2 if kb else 1
            for hp in range(4):
                bk = 4 + hp
                own(bk)
                for j in range(2):
                    for w in range(2 - nc_, 2):
                        t = pe.do(lambda e, bk=bk, j=j, w=w, hp=hp: e.transpose(
                            bank(bk)[:, 256 * j + w * P:256 * j + w * P + P], E[:, 2 * hp + j, w * P:w * P + P], identF[:]))
                act.need(t, prev.get("av"))
                dve.need(t, prev.get("av"))
                q = act if hp % 2 == 0 else dve
                cp = (lambda e, o, i: e.copy(o, i)) if q is act else (lambda e, o, i: e.tensor_copy(o, i))
                a = q.do(lambda e, cp=cp, bk=bk, hp=hp, lo=lo: cp(e, ET[:, 2 * hp:2 * hp + 2, lo:256],
                                                                  bank(bk).rearrange("p (h n) -> p h n", h=2)[:, :, lo:256]))
                free(bk, a)
                pe.need(a) if hp == 3 else None
                if hp == 2:
                    a2 = a
            pe.need(a2, a_v)
            prev["te"] = t
            own(3)
            for h in range(8):
                for w in range(2 - nc_, 2):
                    t = pe.do(lambda e, h=h, w=w, kb=kb, nc_=nc_: e.matmul(
                        bank(3)[:, h * DH:(h + 1) * DH], ET[:, h, w * P:w * P + P], V[:, kb - 1 + w, h * DH:(h + 1) * DH],
                        start=(w == 2 - nc_), stop=(w == 1)))
            prev["av1"], prev["av"] = prev.get("av"), t
            dve.need(t, rz, prev.get("to"))
            d = dve.do(lambda e: e.tensor_tensor(O.rearrange("p (h d) -> p h d", h=8),
                                                 bank(3).rearrange("p (h d) -> p h d", h=8),
                                                 rZ.unsqueeze(2).broadcast_to([P, 8, DH]), ALU.mult))
            free(3, d)
            pe.need(d)
            own(3)
            for c in range(4):
                t = pe.do(lambda e, c=c: e.transpose(bank(3)[:, c * P:(c + 1) * P], O[:, c * P:(c + 1) * P], identF[:]))
            prev["to"] = t
            act.need(t, prev.get("wo"))
            a = act.do(lambda e: e.copy(OT, bank(3)))
            free(3, a)
            pe.need(a)
            own(3)
            for c in range(4):
                t = pe.do(lambda e, c=c: e.matmul(bank(3)[:, 0:P], OT[:, c * P:(c + 1) * P], wo[:, c, :],
                                                  start=(c == 0), stop=(c == 3)))
            prev["wo"] = t
            dve.need(t, m_X, *mh)
            d = dve.do(lambda e, k=k: e.tensor_tensor(X[:, k, :], X[:, k, :], bank(3)[:, 0:P], ALU.add))
            free(3, d)
        m_X = d
        htfree = [prev["wo"]]
        mh = shifted(m_X, hfree)
        dve.need(mh[1])
        m = layernorm(H, H, lambda k: mh[0], gam=lgb[:, 0, :], m_gam=None, bet=lgb[:, 1, :])
        t_h, m_HT = transposed([m[15]], htfree)
        dve.need(t_h)
        zs = [dve.do(lambda e, b=b: e.memset(H[0:1, 8 * b, 64:128], 0.0)) for b in range(NB)]
        hfree = [t_h] + zs
        prev = dict()
        for k in range(16):
            pe.need(m_HT)
            b0 = 2 * (k % 2)
            mq = []
            for c in range(2):
                own(b0 + c)
                mq.append(pe.do(lambda e, c=c, k=k, b0=b0: e.matmul(bank(b0 + c)[:, 0:HID], HT[:, k * P:(k + 1) * P],
                                                                    w1[:, c * HID:(c + 1) * HID], start=True, stop=True)))
            dve.need(mq[1], prev.get("tp"))
            d1 = dve.do(lambda e, b0=b0: e.tensor_tensor(G, bank(b0 + 1)[:, 0:HID], b1[:, HID:2 * HID], ALU.add))
            free(b0 + 1, d1)
            d2 = dve.do(lambda e, b0=b0: e.tensor_tensor(A, bank(b0)[:, 0:HID], b1[:, 0:HID], ALU.add))
            free(b0, d2)
            act.need(d1)
            a = act.do(lambda e: e.activation(G, G, ACT.Gelu))
            dve.need(a, d2)
            d = dve.do(lambda e: e.tensor_tensor(G, G, A, ALU.mult))
            pe.need(d)
            own(4)
            for c in range(3):
                n = min(P, HID - c * P)
                t = pe.do(lambda e, c=c, n=n: e.transpose(bank(4)[0:n, c * P:(c + 1) * P], G[:, c * P:c * P + n], identF[:]))
            prev["tp"] = t
            act.need(t, prev.get("w2"))
            a = act.do(lambda e: e.copy(PT[:, 0:2, :], bank(4)[:, 0:256].rearrange("p (c n) -> p c n", c=2)))
            a = act.do(lambda e: e.copy(PT[0:85, 2, :], bank(4)[0:85, 256:384]))
            free(4, a)
            pe.need(a)
            own(5)
            for c in range(3):
                n = min(P, HID - c * P)
                t = pe.do(lambda e, c=c, n=n: e.matmul(bank(5)[:, 0:P], PT[0:n, c, :], w2[0:n, c, :],
                                                       start=(c == 0), stop=(c == 2)))
            prev["w2"] = t
            dve.need(t)
            d = dve.do(lambda e, k=k: e.tensor_tensor(X[:, k, :], X[:, k, :], bank(5)[:, 0:P], ALU.add))
            free(5, d)
            dve.need(d)
            d = dve.do(lambda e, k=k: e.tensor_tensor(X[:, k, :], X[:, k, :], lgb[:, 2, :], ALU.add))
        m_X = d
        rel = [d, t]
    m = layernorm(X, X, lambda k: m_X)
    dve.need(m[15])
    d = dve.do(lambda e: e.tensor_tensor(x0[:], x0[:], X, ALU.add))
    s_out = sem("s_out")
    sp.need(d)
    sp.dma(lambda e: e.dma_start(OUT.rearrange("b (k p) d -> p (b k) d", p=P), x0[:]), s_out, 16)
    sp.ops.append((s_out, 16))


def constants():
    i = np.arange(P)
    causal = np.zeros((2, P, P), np.float32)
    causal[0] = np.where(i[None, :] <= i[:, None], 0.0, -BIG)
    causal[1] = causal[0].T
    j = np.arange(2 * P) - P
    diff = i[:, None] - j[None, :]
    band = np.where((diff >= 0) & (diff <= 64), 0.0, -BIG).astype(np.float32)
    f = np.float32
    hidx = np.arange(0, DH, 2, dtype=f)
    inv = (f(1.0) / np.power(f(10000.0), hidx / f(DH))).astype(f)
    t = np.arange(NT, dtype=f)
    fr = (t[:, None] * inv[None, :]).astype(f)
    fr = np.concatenate([fr, fr], -1).astype(np.float64)
    base = ((hidx + f(0.4 * DH)) / f(1.4 * DH)).astype(f)
    power = ((t - NT // 2) / f(32.0)).astype(f)
    sc = base[None, :].astype(np.float64) ** power[:, None].astype(np.float64)
    sc = np.concatenate([sc, sc], -1)
    sign = np.concatenate([-np.ones(DH // 2), np.ones(DH // 2)])
    cos, sin = np.cos(fr), np.sin(fr) * sign
    rot = np.stack([cos * sc, sin * sc, cos / sc, sin / sc]).astype(f)
    return {"c_ident": np.eye(P, dtype=f), "c_causal": causal, "c_band": band, "c_rot": rot}


def kernel(**inputs):
    import concourse.bacc as bacc
    from concourse.bass_utils import run_bass_kernel_spmd

    nc = bacc.Bacc("TRN2", target_bir_lowering=False, num_devices=1)
    arrays = {k: np.ascontiguousarray(v) for k, v in inputs.items()}
    arrays.update(constants())
    I = {k: nc.dram_tensor("in_" + k, a.shape, mybir.dt.from_np(a.dtype), kind="ExternalInput").ap() for k, a in arrays.items()}
    out = nc.dram_tensor("out_0", (NB, NT, DM), F32, kind="ExternalOutput").ap()
    program(nc, I, out)
    r = run_bass_kernel_spmd(nc, [{"in_" + k: a for k, a in arrays.items()}], core_ids=[0])
    return r.results[0]["out_0"]
```

```python
from contextlib import ExitStack

import numpy as np

import concourse.bass as bass
from concourse import mybir

F32 = mybir.dt.float32
F32R = mybir.dt.float32r
BF16 = mybir.dt.bfloat16
ACT = mybir.ActivationFunctionType
ALU = mybir.AluOpType
AX = mybir.AxisListType

P = 128
NB, NT, DM = 2, 1024, 128
NBLK = NT // P
HA, DH = 16, 64
HB = 8
INNER = HB * DH
HID = 341
DEPTH = 2
EPS = 1e-5
BIG = float(2.0 ** 100)


class Eng:

    def __init__(self, sem):
        self.sem, self.n, self.ops, self.seen = sem, 0, [], {}

    def need(self, *marks):
        for m in marks:
            if m is not None and self.seen.get(id(m[0]), 0) < m[1]:
                self.seen[id(m[0])] = m[1]
                self.ops.append((m[0], m[1]))

    def do(self, fn, sig=True):
        if sig:
            self.n += 1
        self.ops.append((fn, sig))
        return (self.sem, self.n) if sig else None

    def dma(self, fn, sem, count):
        self.ops.append((fn, sem, count))

    def emit(self, eng):
        for op in self.ops:
            if len(op) == 3:
                op[0](eng).then_inc(op[1], 16)
            elif callable(op[0]):
                ins = op[0](eng)
                if op[1]:
                    ins.then_inc(self.sem, 1)
            else:
                eng.wait_ge(op[0], op[1])


def program(nc, I, OUT):
    with ExitStack() as ctx:
        cnt = [0]
        scope = [ctx]

        def sb(shape, dt=F32):
            cnt[0] += 1
            return scope[0].enter_context(nc.sbuf_tensor(f"t{cnt[0]}", shape, dt))

        def ar(n):
            return sb([P, n])[:, :]

        def sem(name):
            return ctx.enter_context(nc.semaphore(name))

        pe, dve, act, pool, sp = (Eng(sem("s_" + n)) for n in ("pe", "dve", "act", "pool", "sp"))
        PS = ctx.enter_context(nc.psum_tensor("PS", [P, 8 * 512], F32))
        bank_free = [[] for _ in range(8)]

        def bank(k, n=1):
            return PS[:, k * 512:(k + n) * 512]

        def own(k, n=1):
            for b in range(k, k + n):
                pe.need(*bank_free[b])

        def free(k, *marks):
            bank_free[k] = list(marks)

        nload = [0]

        def load(dst, src, after=()):
            s = sem(f"ld{nload[0]}")
            nload[0] += 1
            sp.need(*after)
            sp.dma(lambda e: e.dma_start(dst, src), s, 16)
            return (s, 16)

        x0 = sb([P, 16, DM])
        x_tiles = I["L0_attn_x"].rearrange("b (k p) d -> p (b k) d", p=P)
        m_x = load(x0[:], x_tiles)
        identF = sb([P, P])
        gam_in = sb([P, DM])
        cm = sb([P, 2, P])
        m_id = load(identF[:], I["c_ident"])
        m_gin = load(gam_in[:], I["L0_attn_gamma_in"].rearrange("(a d) -> a d", a=1).broadcast_to([P, DM]))
        m_cm = load(cm[:], I["c_causal"].rearrange("a p d -> p a d"))
        identR = sb([P, P], F32R)
        identB = sb([P, P], BF16)
        half = sb([P, 16])
        fsc = sb([P, 2])
        st6 = sb([P, 16, 6])
        mv = sb([P, 16, 2])
        rs = sb([P, 16])
        first = ExitStack()
        scope[0] = first
        WqD = ar(1024).rearrange("p (h d) -> p h d", h=HA)
        WkD = ar(1024).rearrange("p (h d) -> p h d", h=HA)
        m_wq = [load(WqD, I["L0_attn_Wq"].rearrange("f (h d) -> f h d", h=HA))]
        m_wk = [load(WkD, I["L0_attn_Wk"].rearrange("f (h d) -> f h d", h=HA))]
        WV2 = ar(2048).rearrange("p (h d) -> p h d", h=HA)
        OF = [ar(1024).rearrange("p (k d) -> p k d", k=8) for _ in range(2)]
        Wv = OF[0].rearrange("p k d -> p (k d)")
        m_wv = load(Wv[:], I["L0_attn_Wv"])
        m_wv2 = load(WV2[:, :, 0:DH], I["L0_attn_Wv"].rearrange("f (h d) -> f h d", h=HA))
        WO = ar(2048).rearrange("p (h d) -> p h d", h=HA)
        m_wo = load(WO[0:DH, :, :], I["L0_attn_Wo"].rearrange("(h e) n -> e h n", h=HA))
        w0d = sb([P, P])
        m_z0 = dve.do(lambda e: e.memset(w0d[:], 0.0))
        m_w0d = [load(w0d[t * DH:(t + 1) * DH, t * DH:(t + 1) * DH], I["L0_attn_gnn_w"][0], after=[m_z0]) for t in range(2)]
        WG = sb([66, 130])
        m_wgz = dve.do(lambda e: e.memset(WG[:], 0.0))
        m_wg = [load(WG[:, 0:DH], I["c_ident"][0:66, 0:DH], after=[m_wgz]), load(WG[0:DH, DH:P], I["L0_attn_gnn_w"][0]),
                load(WG[:, P:130], I["c_ident"][0:66, 64:66])]
        WW1 = sb([P, DH])
        m_ww1 = [load(WW1[t * DH:(t + 1) * DH, :], I["L0_attn_gnn_w"][1]) for t in range(2)]
        linw = sb([DH, DH])
        m_lw = load(linw[:], I["L0_attn_lin_w"])
        linb = sb([DH, 1])
        m_lb = load(linb[:], I["L0_attn_lin_b"].rearrange("(d a) -> d a", a=1))
        gb = sb([P, 2, DH])
        m_gb = [load(gb[:, t, :], I["L0_attn_gnn_b"][t:t + 1, :].broadcast_to([P, DH])) for t in range(2)]
        gam_out = sb([P, DM])
        m_gout = load(gam_out[:], I["L0_attn_gamma_out"].rearrange("(a d) -> a d", a=1).broadcast_to([P, DM]))

        cmB = sb([P, 2, P], BF16)
        dve.need(m_id, m_cm)
        m_idR = dve.do(lambda e: e.tensor_copy(identR[:], identF[:]))
        dve.do(lambda e: e.tensor_copy(identB[:], identF[:]))
        m_cmB = dve.do(lambda e: e.tensor_copy(cmB[:], cm[:]))
        m_half = pool.do(lambda e: e.memset(half[:], -0.5))

        def layernorm(dst, src, m_src, ks=range(16), gam=None, m_gam=None, bet=None):
            ks = list(ks)
            a, z = ks[0], ks[-1] + 1
            for k in ks:
                dve.need(m_src(k))
                m = dve.do(lambda e, k=k: e.bn_stats(st6[:, k, :], src[:, k, :]))
            dve.need(m)
            for k in ks:
                m = dve.do(lambda e, k=k: e.bn_aggr(mv[:, k, :], st6[:, k, :]))
            dve.need(m)
            m = dve.do(lambda e: e.tensor_scalar(rs[:, a:z], mv[:, a:z, 1], EPS, None, ALU.add))
            pool.need(m, m_half)
            m = pool.do(lambda e: e.tensor_tensor(rs[:, a:z], rs[:, a:z], half[:, a:z], ALU.pow))
            dve.need(m, m_gam)
            out = {}
            for k in ks:
                out[k] = dve.do(lambda e, k=k: e.tensor_scalar(dst[:, k, :], src[:, k, :], mv[:, k, 0:1], rs[:, k:k + 1],
                                                               ALU.subtract, ALU.mult))
            for t, op in ((gam, ALU.mult), (bet, ALU.add)):
                if t is not None:
                    dve.need(out[ks[-1]])
                    m = dve.do(lambda e, t=t, op=op: e.tensor_tensor(dst[:, a:z, :], dst[:, a:z, :],
                                                                    t[:].unsqueeze(1).broadcast_to([P, z - a, DM]), op))
                    out = {k: m for k in ks}
            return out

        xn = ar(2048).rearrange("p (k d) -> p k d", k=16)
        xnT = ar(2048)
        m = layernorm(xn, x0, lambda k: m_x)
        m = layernorm(xn, xn, lambda k: m[15], gam=gam_in, m_gam=m_gin)
        for g in range(4):
            own(g)
            pe.need(m[15], m_id)
            for r in range(4):
                t = pe.do(lambda e, g=g, r=r: e.transpose(bank(g)[:, r * P:(r + 1) * P], xn[:, 4 * g + r, :], identF[:]), r == 3)
            act.need(t)
            m_xnT = act.do(lambda e, g=g: e.copy(xnT[:, g * 512:(g + 1) * 512], bank(g)))
            free(g, m_xnT)

        WvT = xn.rearrange("p k d -> p (k d)")
        for g in range(2):
            own(4 + g)
            pe.need(m_wv, m_xnT)
            for r in range(4):
                t = pe.do(lambda e, g=g, r=r: e.transpose(bank(4 + g)[:, r * P:(r + 1) * P],
                                                          Wv[:, (4 * g + r) * P:(4 * g + r + 1) * P], identF[:]), r == 3)
            act.need(t)
            m_wvT = act.do(lambda e, g=g: e.copy(WvT[:, g * 512:(g + 1) * 512], bank(4 + g)))
            free(4 + g, m_wvT)
        pe.need(m_wvT, *m_w0d)
        for g in range(2):
            own(6 + g)
            for r in range(4):
                t = pe.do(lambda e, g=g, r=r: e.matmul(bank(6 + g)[:, r * P:(r + 1) * P],
                                                       WvT[:, (4 * g + r) * P:(4 * g + r + 1) * P], w0d[:],
                                                       start=True, stop=True), r == 3)
            act.need(t)
            m_wv2p = act.do(lambda e, g=g: e.copy(WV2[:, 8 * g:8 * g + 8, DH:P],
                                                  bank(6 + g).rearrange("p (h d) -> p h d", h=8)))
            free(6 + g, m_wv2p)
        LW = sb([DH, P])
        LBc = sb([DH, P])
        m_lz = dve.do(lambda e: e.memset(LW[:], 0.0))
        own(0)
        pe.need(m_lw)
        t = pe.do(lambda e: e.transpose(bank(0)[0:DH, 0:DH], linw[:], identF[0:DH, 0:DH]))
        dve.need(t, m_lb, m_lz)
        m_LW = dve.do(lambda e: e.tensor_copy(LW[:, DH:P], bank(0)[0:DH, 0:DH]))
        m_LBc = dve.do(lambda e: e.tensor_copy(LBc[:], linb[:].broadcast_to([DH, P])))
        free(0, m_LW)
        pe.need(m_LW, m_LBc, m_wo)
        for g in range(4):
            own(g)
            t = pe.do(lambda e, g=g: e.matmul(bank(g), LW[:], WO[0:DH, 4 * g:4 * g + 4, :], start=True, stop=True))
            act.need(t)
            m_WO = act.do(lambda e, g=g: e.copy(WO[DH:P, 4 * g:4 * g + 4, :],
                                                bank(g)[DH:P].rearrange("p (h d) -> p h d", h=4)))
            free(g, m_WO)
        own(4)
        for h in range(HA):
            t = pe.do(lambda e, h=h: e.matmul(bank(4)[:, 0:P], LBc[:], WO[0:DH, h, :], start=(h == 0), stop=(h == HA - 1)),
                      h == HA - 1)
        ylin = sb([P, P])
        dve.need(t)
        m_ylin = dve.do(lambda e: e.tensor_copy(ylin[:], bank(4)[:, 0:P]))
        free(4, m_ylin)

        R3 = 2
        Q1 = [sb([P, NT], F32R) for _ in range(R3)]
        K1 = [sb([P, NT], F32R) for _ in range(R3)]
        K2 = [sb([66, NT], F32R) for _ in range(R3)]
        Q2 = [sb([66, NT], F32R) for _ in range(R3)]
        vB = [ar(512).rearrange("p (k d) -> p k d", k=8) for _ in range(R3)]
        vW = [ar(512).rearrange("p (k d) -> p k d", k=8) for _ in range(R3)]
        VH = [sb([P, 8, 66], F32R) for _ in range(R3)]
        VL = [sb([P, 8, 66], F32R) for _ in range(R3)]
        WD = [sb([P, 2, 2, DH]) for _ in range(2)]
        NM = [sb([P, 8, 66], F32R) for _ in range(2)]
        nm = [sb([P, 8]) for _ in range(2)]
        EC = 4608
        Eh = sb([P, EC], F32R)
        El = sb([P, EC], F32R)
        NS = 3
        Es = ar(NS * 512).rearrange("p (s n) -> p s n", s=NS)
        dscr = ar(128)
        eD = [sb([P, 8]) for _ in range(2)]
        RT = sb([66, NT])
        RT2 = ar(NT)
        gZ = [sb([P, 4, 8]) for _ in range(2)]
        t1 = ar(512).rearrange("p (k d) -> p k d", k=8)
        fF = [ar(512).rearrange("p (k d) -> p k d", k=8) for _ in range(2)]
        fB = ar(512).rearrange("p (k d) -> p k d", k=8)
        gf = ar(512).rearrange("p (k d) -> p k d", k=8)
        F2 = sb([P, 8, P], F32R)
        G2 = sb([P, 8, P], F32R)
        OFT = ar(1024)
        Y = xn
        ini = sb([P, 2, 66])
        m_i0 = dve.do(lambda e: e.memset(ini[:, 0, :], 0.0))
        m_i1 = dve.do(lambda e: e.memset(ini[:, 1, :], 1.0))
        dve.need(m_i0, m_i1)
        ini_m = []
        for i in range(R3):
            ini_m.append(dve.do(lambda e, i=i: e.tensor_copy(VL[i][:, :, 64:66], ini[:, 0:1, 0:2].broadcast_to([P, 8, 2]))))
            ini_m.append(dve.do(lambda e, i=i: e.tensor_copy(VH[i][:, :, 64:66], ini[:, 1:2, 0:2].broadcast_to([P, 8, 2]))))
            ini_m.append(dve.do(lambda e, i=i: e.tensor_copy(K2[i][64:66, :], ini[64:66, 1, 0:1].broadcast_to([2, NT]))))
        for i in range(2):
            ini_m.append(dve.do(lambda e, i=i: e.tensor_copy(NM[i][:, :, 0:64], ini[:, 0:1, 0:64].broadcast_to([P, 8, 64]))))
        m_ini = ini_m[-1]
        dve.need(m_ylin, m_wv2p)
        for b in range(NB):
            m_Y = dve.do(lambda e, b=b: e.tensor_copy(Y[:, 8 * b:8 * b + 8, :], ylin[:].unsqueeze(1).broadcast_to([P, 8, P])))

        tiles = []
        off = 0
        for c in range(2):
            for jb in range(4 * c + 4):
                i0 = max(c * 512, jb * P)
                n = (c + 1) * 512 - i0
                tiles.append((c, jb, i0, n, off))
                off += n
        assert off == EC
        NH = NB * HA
        S = [dict() for _ in range(NH)]

        def f32(ap):
            return ap.bitcast(F32)

        def old(t, key):
            return S[t][key] if t >= 0 else None

        def widen(t):
            if t >= NH:
                return
            pool.need(*m_wq, *m_wk, old(t - 2, "proj"))
            for i, W in enumerate((WkD, WqD)):
                S[t]["wd"] = pool.do(lambda e, i=i, W=W: e.tensor_copy(
                    WD[t % 2][:, i, :, :], W[:, t % HA:t % HA + 1, :].broadcast_to([P, 2, DH])))

        def proj(t):
            b, h = divmod(t, HA)
            r, s = t % R3, S[t]
            pe.need(m_xnT, m_WO, s["wd"])
            later = []
            for i, (which, T1, b0) in enumerate((("k", K1[r], 6), ("q", Q1[r], 2))):
                sc = 0.125 if which == "q" else 1.0
                for c in range(2):
                    bk = b0 + c
                    sl = slice(c * 512, (c + 1) * 512)
                    own(bk)
                    mm = pe.do(lambda e, i=i, bk=bk, c=c: e.matmul(bank(bk), WD[r][:, i, :, :].rearrange("p t d -> p (t d)"),
                                                                   xnT[:, b * NT + c * 512:b * NT + (c + 1) * 512],
                                                                   start=True, stop=True))
                    s["proj"] = mm
                    act.need(mm, old(t - R3, "av"), old(t - R3, "smax_pe"), m_ini)
                    mh = act.do(lambda e, T1=T1, sl=sl, bk=bk, sc=sc: e.activation(T1[:, sl], bank(bk), ACT.Copy, scale=sc))
                    later.append((which, T1, bk, sl, mm, mh))

            def lower():
                for which, T1, bk, sl, mm, mh in later:
                    dve.need(mm, mh, old(t - R3, "av"))
                    if which == "k":
                        ml = dve.do(lambda e, T1=T1, sl=sl, bk=bk: e.tensor_tensor(K2[r][0:64, sl], bank(bk)[0:64, :],
                                                                                   f32(T1[0:64, sl]), ALU.subtract))
                        s["kl"] = ml
                    else:
                        ml = dve.do(lambda e, T1=T1, sl=sl, bk=bk: e.scalar_tensor_tensor(
                            T1[64:128, sl], bank(bk)[64:128, :], 0.125, f32(T1[64:128, sl]), ALU.mult, ALU.subtract))
                        s["ql"] = ml
                        pool.need(mh, old(t - R3, "av"))
                        s["q2"] = pool.do(lambda e, sl=sl, T1=T1: e.tensor_copy(Q2[r][0:64, sl], f32(T1[0:64, sl])))
                    free(bk, ml)
            return lower

        def projv(t):
            b, h = divmod(t, HA)
            r, s = t % R3, S[t]
            pe.need(m_xnT, m_wv2p, m_wv2)
            for c in range(2):
                bk = c
                own(bk)
                for k in range(4):
                    mm = pe.do(lambda e, bk=bk, c=c, k=k: e.matmul(bank(bk)[:, k * P:(k + 1) * P],
                                                                   xnT[:, b * NT + (4 * c + k) * P:b * NT + (4 * c + k + 1) * P],
                                                                   WV2[:, h, :], start=True, stop=True), k == 3)
                pv = bank(bk).rearrange("p (k d) -> p k d", k=4)
                ks = slice(4 * c, 4 * c + 4)
                act.need(mm, old(t - R3, ("n2", 1)), old(t - R3, "av"))
                act.do(lambda e, pv=pv, ks=ks: e.copy(vW[r][:, ks, :], pv[:, :, DH:P]), False)
                a3 = act.do(lambda e, pv=pv, ks=ks: e.copy(VH[r][:, ks, 0:DH], pv[:, :, 0:DH]))
                dve.need(a3, *m_gb, old(t - R3, ("n6", 1)))
                s["vl"] = dve.do(lambda e, pv=pv, ks=ks: e.tensor_tensor(VL[r][:, ks, 0:DH], pv[:, :, 0:DH],
                                                                         f32(VH[r][:, ks, 0:DH]), ALU.subtract))
                s["vb"] = dve.do(lambda e, pv=pv, ks=ks: e.tensor_tensor(vB[r][:, ks, :], pv[:, :, 0:DH],
                                                                         gb[:, 0:1, :].broadcast_to([P, 4, DH]), ALU.add))
                free(bk, s["vb"])
                s["va"] = a3

        def smax(t, ib):
            r, s = t % R3, S[t]
            pe.need(s["ql"], s["kl"], m_cmB)
            if True:
                w = (ib + 1) * P
                b0 = 0 if ib >= 4 else ib % 2
                nb = 2 if ib >= 4 else 1
                own(b0, nb)
                for c in range(nb):
                    lo, hi = c * 512, min(w, (c + 1) * 512)
                    pe.do(lambda e, b0=b0, c=c, lo=lo, hi=hi, ib=ib, last=(hi == w): e.matmul(
                        bank(b0 + c)[:, 0:hi - lo], Q1[r][:, ib * P:(ib + 1) * P], K1[r][:, lo:hi],
                        start=True, stop=not last), False)
                d0 = (ib * P) % 512
                mm = pe.do(lambda e, bb=b0 + nb - 1, d0=d0: e.matmul(bank(bb)[:, d0:d0 + P], identB[:], cmB[:, 0, :],
                                                                     start=False, stop=True))
                dve.need(mm, old(t - 2, "mrow_pe"))
                md = dve.do(lambda e, b0=b0, nb=nb, w=w, ib=ib: e.tensor_reduce(
                    nm[t % 2][:, ib:ib + 1], bank(b0, nb)[:, 0:w], AX.X, ALU.max, negate=True))
                for k in range(nb):
                    free(b0 + k, md)
            s["smax_pe"] = mm
            if ib < 7:
                return
            dve.need(md)
            m1 = dve.do(lambda e: e.tensor_copy(NM[t % 2][:, :, 64], nm[t % 2][:]))
            dve.need(m1)
            s["nm"] = dve.do(lambda e: e.tensor_tensor(NM[t % 2][:, :, 65], nm[t % 2][:], f32(NM[t % 2][:, :, 64]), ALU.subtract))

        def mrow(t):
            r, s = t % R3, S[t]
            pe.need(s["nm"], m_idR)
            for c in range(2):
                own(6 + c)
                for k in range(4):
                    mm = pe.do(lambda e, c=c, k=k: e.matmul(bank(6 + c)[0:66, k * P:(k + 1) * P], NM[t % 2][:, 4 * c + k, :],
                                                            identR[:], start=True, stop=True), k == 3)
                act.need(mm)
                s["q2m"] = act.do(lambda e, c=c: e.copy(Q2[r][64:66, c * 512:(c + 1) * 512], bank(6 + c)[64:66, :]))
                free(6 + c, s["q2m"])
            s["mrow_pe"] = mm

        est = [None] * NS
        enum = [0]

        def av(t, k):
            r, s = t % R3, S[t]
            c, jb, i0, n, o = tiles[k]
            if jb == 0:
                own(4)
            pe.need(s["E"][k], s["vl"], s["va"])
            dst = bank(4)[0:66, i0 - c * 512:512]
            pe.do(lambda e: e.matmul(dst, VH[r][:, jb, :], Eh[:, o:o + n], start=(jb == 0), stop=False), False)
            pe.do(lambda e: e.matmul(dst, VL[r][:, jb, :], Eh[:, o:o + n], start=False, stop=False), False)
            mm = pe.do(lambda e: e.matmul(dst, VH[r][:, jb, :], El[:, o:o + n], start=False, stop=(jb == 4 * c + 3)))
            if jb == 4 * c + 3:
                act.need(mm, old(t - 1, ("g0", c)))
                s["rt", c] = act.do(lambda e: e.copy(RT[:, c * 512:(c + 1) * 512], bank(4)[0:66, :]))
                free(4, s["rt", c])
            s["av"] = mm

        def scores(t, k):
            r, u, s = t % R3, t % 2, S[t]
            c, jb, i0, n, o = tiles[k]
            pe.need(s["q2m"], s["q2"], s["kl"], s["ql"])
            bk = 2 + k % 2
            own(bk)
            diag = jb >= 4 * c
            pe.do(lambda e: e.matmul(bank(bk)[:, 0:n], K1[r][:, jb * P:(jb + 1) * P], Q1[r][:, i0:i0 + n],
                                     start=True, stop=False), False)
            mm = pe.do(lambda e: e.matmul(bank(bk)[:, 0:n], K2[r][:, jb * P:(jb + 1) * P], Q2[r][:, i0:i0 + n],
                                          start=False, stop=not diag), not diag)
            if diag:
                mm = pe.do(lambda e: e.matmul(bank(bk)[:, 0:P], identB[:], cmB[:, 1, :], start=False, stop=True))
            q = enum[0] % NS
            enum[0] += 1
            act.need(mm, est[q], S[t - 1]["l2t"][k] if t else None)
            me = act.do(lambda e: e.activation(Es[:, q, 0:n], bank(bk)[:, 0:n], ACT.Exp))
            mh = act.do(lambda e: e.activation(Eh[:, o:o + n], bank(bk)[:, 0:n], ACT.Exp))
            free(bk, mh)
            dve.need(me)
            if diag:
                dve.need(old(t - 2, ("gz", 1)), s.get("e") or old(t - 1, "e"))
                s["e"] = dve.do(lambda e: e.scalar_tensor_tensor(
                    dscr[:, 0:P], Es[:, q, 0:P], 1.0, identF[:], ALU.mult, ALU.mult, accum_out=eD[u][:, jb:jb + 1]))
                s["e", c] = s["e"]
            dve.need(mh)
            est[q] = dve.do(lambda e: e.tensor_tensor(El[:, o:o + n], Es[:, q, 0:n], f32(Eh[:, o:o + n]), ALU.subtract))
            s.setdefault("E", {})[k] = est[q]

        est = [None] * NS
        enum = [0]

        def bc(ap):
            return ap.unsqueeze(2).broadcast_to([P, 8, DH])

        def graph1(t, c, b0):
            r, u, s = t % R3, t % 2, S[t]
            pe.need(s["rt", c], *m_wg)
            own(b0, 2)
            for k in range(4):
                mm = pe.do(lambda e, k=k: e.matmul(bank(b0 + k // 2)[:, 130 * (k % 2):130 * (k % 2) + 130],
                                                   RT[0:66, (4 * c + k) * P:(4 * c + k + 1) * P], WG[:],
                                                   start=True, stop=True), k == 3)
            s["g0", c] = mm
            ks = slice(4 * c, 4 * c + 4)
            pv = bank(b0, 2).rearrange("p (b x) -> p b x", b=2)[:, :, 0:260].rearrange("p b (k d) -> p b k d", k=2)
            g = gZ[u]

            def four(ap):
                return ap.rearrange("p (b k) d -> p b k d", b=2)

            def col(i):
                return four(g[:, i, ks].unsqueeze(2).broadcast_to([P, 4, DH]))

            dve.need(mm, s["e", c], old(t - 2, "p1"))
            a = dve.do(lambda e: e.tensor_copy(g[:, 0, ks].rearrange("p (b k) -> p b k", b=2), pv[:, :, :, 128]))
            dve.need(a)
            a = dve.do(lambda e: e.tensor_tensor(g[:, 1, ks], g[:, 0, ks], eD[u][:, ks], ALU.subtract))
            pool.need(a, s["va"], old(t - 1, ("n6", c)), old(t - 1, ("ge1", c)))
            n2 = pool.do(lambda e: e.tensor_tensor(t1[:, ks, :], vW[r][:, ks, :], g[:, 1, ks].unsqueeze(2).broadcast_to([P, 4, DH]),
                                                   ALU.mult))
            dve.need(a)
            b_ = dve.do(lambda e: e.tensor_tensor(g[:, 3, ks], g[:, 0, ks], g[:, 1, ks], ALU.add))
            c_ = dve.do(lambda e: e.reciprocal(g[:, 2, ks], g[:, 0, ks]))
            dve.need(b_)
            d_ = dve.do(lambda e: e.reciprocal(g[:, 3, ks], g[:, 3, ks]))
            s["gz", c] = d_
            dve.need(n2)
            n3 = dve.do(lambda e: e.tensor_tensor(four(t1[:, ks, :]), four(t1[:, ks, :]), pv[:, :, :, DH:P], ALU.add))
            dve.need(n3, d_)
            n4 = dve.do(lambda e: e.tensor_tensor(t1[:, ks, :], t1[:, ks, :], g[:, 3, ks].unsqueeze(2).broadcast_to([P, 4, DH]),
                                                  ALU.mult))
            dve.need(n4, s["vb"])
            n6 = dve.do(lambda e: e.tensor_tensor(t1[:, ks, :], t1[:, ks, :], vB[r][:, ks, :], ALU.add))
            dve.need(c_, old(t - 2, "ofT"))
            n1 = dve.do(lambda e: e.tensor_tensor(four(OF[u][:, ks, 0:DH]), pv[:, :, :, 0:DH], col(2), ALU.mult))
            free(b0, n1)
            free(b0 + 1, n1)
            s["o1"] = n1
            s["n2", c], s["n6", c] = n2, n6

        def feats(t, c):
            u, s = t % 2, S[t]
            ks = slice(4 * c, 4 * c + 4)
            used = S[t - 1]["l2t"][7 if c == 0 else 11] if t else None
            act.need(s["n6", c], old(t - 2, "fuse"))
            s["ge1", c] = act.do(lambda e: e.activation(fF[u][:, ks, :], t1[:, ks, :], ACT.Gelu))
            act.need(s["ge1", c], used)
            a = act.do(lambda e: e.copy(F2[:, ks, 0:DH], fF[u][:, ks, :]))
            pool.need(s["ge1", c], old(t - 1, ("gl", c)))
            p = pool.do(lambda e: e.tensor_tensor(gf[:, ks, :], fF[u][:, ks, :], gZ[u][:, 1, ks].unsqueeze(2).broadcast_to([P, 4, DH]),
                                                  ALU.mult))
            dve.need(a, used)
            s["f2", c] = dve.do(lambda e: e.tensor_tensor(F2[:, ks, DH:P], fF[u][:, ks, :], f32(F2[:, ks, 0:DH]), ALU.subtract))

            def rest():
                act.need(p, old(t - 1, ("l2", c)))
                a2 = act.do(lambda e: e.copy(G2[:, ks, 0:DH], gf[:, ks, :]))
                dve.need(a2, p)
                s["gl", c] = dve.do(lambda e: e.tensor_tensor(G2[:, ks, DH:P], gf[:, ks, :], f32(G2[:, ks, 0:DH]), ALU.subtract))
            return rest

        def graph2(t, k):
            s = S[t]
            c, jb, i0, n, o = tiles[k]
            pe.need(s["f2", jb // 4])
            if jb == 0:
                own(5)
            dst = bank(5)[:, i0 - c * 512:512]
            pe.do(lambda e: e.matmul(dst, F2[:, jb, :], Eh[:, o:o + n], start=(jb == 0), stop=False), False)
            s.setdefault("l2t", {})[k] = pe.do(lambda e: e.matmul(dst, F2[:, jb, :], El[:, o:o + n], start=False, stop=False))
            if jb == 4 * c + 3:
                pe.need(s["gl", c])
                for i in range(4):
                    mm = pe.do(lambda e, i=i: e.matmul(bank(5)[:, i * P:(i + 1) * P], G2[:, 4 * c + i, :], identR[:],
                                                       start=False, stop=(i == 3)), i == 3)
                act.need(mm, old(t - 1, "r2w"))
                s["rt2"] = act.do(lambda e: e.copy(RT2[:, c * 512:(c + 1) * 512], bank(5)))
                free(5, s["rt2"])
                s["l2", c] = mm

        def graph2b(t):
            u, s = t % 2, S[t]
            own(5)
            pe.need(s["rt2"], *m_ww1)
            for k in range(8):
                mm = pe.do(lambda e, k=k: e.matmul(bank(5)[:, k * DH:(k + 1) * DH], RT2[:, k * P:(k + 1) * P], WW1[:],
                                                   start=True, stop=True), k == 7)
            s["r2w"] = mm
            pool.need(s["ge1", 0], s["ge1", 1], old(t - 1, "p2"))
            fb = pool.do(lambda e: e.tensor_tensor(fB, fF[u], gb[:, 1:2, :].broadcast_to([P, 8, DH]), ALU.add))
            s["fuse"] = fb
            dve.need(mm, old(t - 1, "ge2"))
            p1 = dve.do(lambda e: e.tensor_tensor(t3, bank(5).rearrange("p (k d) -> p k d", k=8), bc(gZ[u][:, 3, :]), ALU.mult))
            free(5, p1)
            s["p1"] = p1
            dve.need(p1, fb)
            s["p2"] = dve.do(lambda e: e.tensor_tensor(t3, t3, fB, ALU.add))

        def gelu2(t):
            s = S[t]
            act.need(s["p2"], s["o1"])
            s["ge2"] = act.do(lambda e: e.activation(OF[t % 2][:, :, DH:P], t3, ACT.Gelu))

        def tail(t):
            b, h = divmod(t, HA)
            s = S[t]
            pe.need(s["ge2"], s["o1"])
            for c in range(2):
                own(6 + c)
                for k in range(4):
                    mm = pe.do(lambda e, c=c, k=k: e.transpose(bank(6 + c)[:, k * P:(k + 1) * P], OF[t % 2][:, 4 * c + k, :],
                                                               identF[:]), k == 3)
                act.need(mm, old(t - 1, "y"))
                a = act.do(lambda e, c=c: e.copy(OFT[:, c * 512:(c + 1) * 512], bank(6 + c)))
                free(6 + c, a)
            s["ofT"] = mm
            pe.need(a)
            for c in range(2):
                own(2 + c)
                for k in range(4):
                    mm = pe.do(lambda e, c=c, k=k: e.matmul(bank(2 + c)[:, k * P:(k + 1) * P],
                                                            OFT[:, (4 * c + k) * P:(4 * c + k + 1) * P], WO[:, h, :],
                                                            start=True, stop=True), k == 3)
                dve.need(mm, m_Y if t == 0 else S[t - 1]["yd"])
                ks = slice(8 * b + 4 * c, 8 * b + 4 * c + 4)
                d = dve.do(lambda e, c=c, ks=ks: e.tensor_tensor(Y[:, ks, :], Y[:, ks, :],
                                                                 bank(2 + c).rearrange("p (k d) -> p k d", k=4), ALU.add))
                free(2 + c, d)
            s["y"], s["yd"] = mm, d

        t3 = ar(512).rearrange("p (k d) -> p k d", k=8)
        widen(0)
        widen(1)
        proj(0)()
        projv(0)
        for ib in range(8):
            smax(0, ib)
        LAG = 3
        NTL = len(tiles)
        for t in range(NH + 2):
            done = 0 <= t - 1 < NH
            if t < NH:
                mrow(t)
            if done:
                graph1(t - 1, 1, 0)
            if t + 1 < NH:
                lower = proj(t + 1)
            if 0 <= t - 2:
                graph2b(t - 2)
            if done:
                rest = feats(t - 1, 1)
            if 0 <= t - 2:
                gelu2(t - 2)
            if t + 1 < NH:
                lower()
            if done:
                rest()
            if t + 1 < NH:
                projv(t + 1)
                widen(t + 2)
            if 0 <= t - 2:
                tail(t - 2)
            for k in range(NTL + LAG):
                if k < NTL:
                    if done:
                        graph2(t - 1, k)
                    if t < NH:
                        scores(t, k)
                if t + 1 < NH and 0 <= k - 2 < 8:
                    smax(t + 1, k - 2)
                if t < NH and k >= LAG:
                    av(t, k - LAG)
                if t < NH and k == 8:
                    graph1(t, 0, 6)
                if t < NH and k == NTL - 1:
                    rest = feats(t, 0)
                    rest()

        m_y = S[NH - 1]["yd"]
        m = layernorm(Y, Y, lambda k: m_y, gam=gam_out, m_gam=m_gout)
        mm_ = m[15]
        m = layernorm(Y, Y, lambda k: mm_)
        dve.need(m[15])
        m_x1 = dve.do(lambda e: e.tensor_tensor(x0[:], x0[:], Y, ALU.add))

        own(7)
        fence = (pe.do(lambda e: e.transpose(bank(7)[:, 0:P], identF[:], identF[:])), m_x1,
                 act.do(lambda e: e.copy(fsc[:, 0:1], identF[:, 0:1])), pool.do(lambda e: e.memset(fsc[:, 1:2], 0.0)))
        free(7, fence[0])
        for q in (pe, dve, act, pool, sp):
            q.need(*fence)
        first.close()
        scope[0] = ctx
        X = ar(2048).rearrange("p (k d) -> p k d", k=16)
        ffn(nc, I, ctx, locals())
        block = ctx.enter_context(nc.Block())
        block.sync(lambda e: sp.emit(e))
        block.tensor(lambda e: pe.emit(e))
        block.vector(lambda e: dve.emit(e))
        block.scalar(lambda e: act.emit(e))
        block.gpsimd(lambda e: pool.emit(e))


def ffn(nc, I, ctx, g):
    pe, dve, act, pool, sp = (g[n] for n in ("pe", "dve", "act", "pool", "sp"))
    X, x0, ar, load, bank, own, free, sb, layernorm = (g[n] for n in (
        "X", "x0", "ar", "load", "bank", "own", "free", "sb", "layernorm"))
    identF, identB, sem, half, fence, OUT = (g[n] for n in ("identF", "identB", "sem", "half", "fence", "OUT"))
    W3 = 192

    wqkv = ar(1536)
    wo = ar(512).rearrange("p (c n) -> p c n", c=4)
    w1 = ar(2 * HID)
    w2 = ar(384).rearrange("p (c n) -> p c n", c=3)
    tab = ar(4 * 512).rearrange("p (f k s d) -> p f k s d", f=2, k=8, s=2)
    tabl = ar(4 * 512).rearrange("p (f k s d) -> p f k s d", f=2, k=8, s=2)
    qks = ar(4 * DH).rearrange("p (f s d) -> p f s d", f=2, s=2)
    lnp = ar(2)
    b2 = ar(DM)
    b1 = ar(2 * HID)
    H = ar(2048).rearrange("p (k d) -> p k d", k=16)
    HT = ar(2048)
    qr = [ar(1024) for _ in range(2)]
    tm = ar(1024)
    sq = ar(1024)
    ss = [ar(16) for _ in range(3)]
    KT = ar(4 * 1024).rearrange("p (c n) -> p c n", c=4)
    QT = [ar(512).rearrange("p (c n) -> p c n", c=4) for _ in range(2)]
    V = ar(8 * 512).rearrange("p (k n) -> p k n", k=8)
    VP = ar(8 * 512).rearrange("p (k n) -> p k n", k=8)
    E = ar(8 * W3).rearrange("p (h n) -> p h n", h=8)
    ET = ar(8 * 256).rearrange("p (h n) -> p h n", h=8)
    nmx = [ar(8) for _ in range(2)]
    sc8 = [ar(8) for _ in range(2)]
    Z = [ar(8) for _ in range(2)]
    rZ = [ar(8) for _ in range(2)]
    O = ar(512)
    OT = ar(512)
    A = [ar(HID) for _ in range(2)]
    G = [ar(HID) for _ in range(2)]
    PT = [ar(384).rearrange("p (c n) -> p c n", c=3) for _ in range(2)]
    bandF = ar(256)
    band = sb([P, 256], BF16)
    m_band = load(bandF, I["c_band"])
    dve.need(m_band)
    m_bandB = dve.do(lambda e: e.tensor_copy(band[:], bandF))
    m_tab = [load(tab[:, f], I["c_rot"][f].rearrange("(k p) s d -> p k s d", p=P)) for f in range(2)]
    m_h0 = dve.do(lambda e: e.memset(H[:, :, :], 0.0))

    m = layernorm(X, x0, lambda k: None)
    m_X = {k: m[15] for k in range(16)}
    rel = list(fence)
    s_shift = [sem("shift0"), sem("shift1")]
    nsh = [0, 0]

    def shifted(b, m_src, m_free):
        sp.need(m_src, *m_free)
        k0, s_sh = 8 * b, s_shift[b]
        sp.dma(lambda e: e.dma_start(H[1:P, k0:k0 + 8, 64:128], X[0:P - 1, k0:k0 + 8, 64:128]), s_sh, 16)
        sp.dma(lambda e: e.dma_start(H[0:1, k0 + 1:k0 + 8, 64:128], X[P - 1:P, k0:k0 + 7, 64:128]), s_sh, 16)
        nsh[b] += 2
        pool.need(m_src, *m_free)
        d = pool.do(lambda e: e.tensor_copy(H[:, k0:k0 + 8, 0:64], X[:, k0:k0 + 8, 0:64]))
        return [d, (s_sh, 16 * nsh[b])]

    def transposed(m_src, m_free, affine):
        out = {}
        for q in range(4):
            pe.need(*m_src[q // 2])
            own(q)
            for r in range(4):
                t = pe.do(lambda e, q=q, r=r: e.transpose(bank(q)[:, r * P:(r + 1) * P], H[:, 4 * q + r, :], identF[:]), r == 3)
            act.need(t, *m_free)
            if affine:
                a = act.do(lambda e, q=q: e.activation(HT[:, q * 512:(q + 1) * 512], bank(q), ACT.Identity,
                                                       bias=lnp[:, 1:2], scale=lnp[:, 0:1]))
            else:
                a = act.do(lambda e, q=q: e.copy(HT[:, q * 512:(q + 1) * 512], bank(q)))
            free(q, a)
            out.update({4 * q + r: a for r in range(4)})
        return t, out

    zero_rows = [m_h0, m_h0]
    t_h = None
    htfree = []
    last = {}
    for l in range(DEPTH):
        m_w = [load(wqkv, I["L0_ffn_wqkv"][l], after=rel), load(wo, I["L0_ffn_wo"][l].rearrange("(c p) n -> p c n", p=P)),
               load(b2, I["L0_ffn_b2"][l:l + 1, :].broadcast_to([P, DM])),
               load(b1, I["L0_ffn_b1"][l:l + 1, :].broadcast_to([P, 2 * HID]))]
        m_w2 = [load(w1, I["L0_ffn_w1"][l]),
                load(w2[:, 0:2, :], I["L0_ffn_w2"][l][0:256, :].rearrange("(c p) n -> p c n", p=P)),
                load(w2[0:85, 2, :], I["L0_ffn_w2"][l][256:HID, :]),
                load(lnp[:, 0:1], I["L0_ffn_ln_g"][l].rearrange("(d a) -> d a", a=1)),
                load(lnp[:, 1:2], I["L0_ffn_ln_b"][l].rearrange("(d a) -> d a", a=1))]
        m_s = []
        for s, name in enumerate(("L0_ffn_q_scale", "L0_ffn_k_scale")):
            src = I[name][l:l + 1, :]
            m_s += [load(qks[:, 0, s, :], src.broadcast_to([P, DH])),
                    load(qks[:, 1, s, 0:32], src[:, 32:64].broadcast_to([P, 32])),
                    load(qks[:, 1, s, 32:64], src[:, 0:32].broadcast_to([P, 32]))]
        pool.need(*m_tab, *m_s, last.get("rot"))
        for f in range(2):
            for s in range(2):
                m_tl = pool.do(lambda e, s=s, f=f: e.tensor_tensor(tabl[:, f, :, s, :], tab[:, f, :, s, :],
                                                                   qks[:, f, s:s + 1, :].broadcast_to([P, 8, DH]), ALU.mult))
        mh = [shifted(b, m_X[8 * b + 7], [zero_rows[b], t_h]) for b in range(NB)]
        t_h, m_HT = transposed(mh, htfree, False)
        B = [dict() for _ in range(16)]

        def at(k, key):
            return B[k].get(key) if k >= 0 else last.get((key, k))

        def qkv(k):
            s, kb, u = B[k], k % 8, k % 2
            pe.need(m_HT[k], *m_w)
            for c in range(3):
                own(c)
                s["qkv%d" % c] = pe.do(lambda e, c=c: e.matmul(bank(c), HT[:, k * P:(k + 1) * P], wqkv[:, c * 512:(c + 1) * 512],
                                                               start=True, stop=True))
            s["HT"] = s["qkv2"]
            act.need(s["qkv2"], at(k - 1, "ss"), at(k - 7, "av"))
            m_sq = [act.do(lambda e, c=c: e.activation(sq[:, c * 512:(c + 1) * 512], bank(c), ACT.Square)) for c in range(2)]
            a_s = m_sq[1]
            act.do(lambda e: e.copy(V[:, kb, :], bank(2)), False)
            s["v"] = act.do(lambda e: e.copy(VP[0:64, kb, :], bank(2)[64:P, :]))
            free(2, s["v"])
            pv = bank(0, 2).rearrange("p (s h d) -> p s h d", s=2, d=DH)
            r4 = qr[u].rearrange("p (s h d) -> p s h d", s=2, d=DH)
            t4 = tm.rearrange("p (s h d) -> p s h d", s=2, d=DH)
            dve.need(s["qkv1"], m_tl, at(k - 2, "tqk"), at(k - 1, "rot"))
            for i in range(2):
                dve.need(m_sq[i])
                d = dve.do(lambda e, i=i: e.tensor_tensor(r4[:, i], pv[:, i], tabl[:, 0, kb, i:i + 1, :].broadcast_to([P, 8, DH]),
                                                          ALU.mult))
                for hf in range(2):
                    d = dve.do(lambda e, i=i, hf=hf: e.tensor_tensor(
                        t4[:, i, :, 32 * hf:32 * hf + 32], pv[:, i, :, 32 - 32 * hf:64 - 32 * hf],
                        tabl[:, 1, kb, i:i + 1, 32 * hf:32 * hf + 32].broadcast_to([P, 8, 32]), ALU.mult))
                free(i, d)
            w = k % 3
            dve.need(a_s, at(k - 3, "sc8"), at(k - 3, "kn"))
            d2 = dve.do(lambda e: e.tensor_reduce(ss[w], sq.rearrange("p (s d) -> p s d", d=DH), AX.X, ALU.add))
            s["ss"] = d2
            dve.need(d2, d)
            s["rot"] = dve.do(lambda e: e.tensor_tensor(qr[u], qr[u], tm, ALU.add))
            d2 = dve.do(lambda e: e.tensor_scalar(ss[w], ss[w], 1e-24, None, ALU.max))
            pool.need(d2)
            p = pool.do(lambda e: e.tensor_tensor(ss[w], ss[w], half[:], ALU.pow))
            dve.need(p, s["rot"], at(k - 2, "exp"))
            s["kn"] = dve.do(lambda e: e.tensor_tensor(r4[:, 1], r4[:, 1], ss[w][:, 8:16].unsqueeze(2).broadcast_to([P, 8, DH]),
                                                       ALU.mult))
            s["sc8"] = dve.do(lambda e: e.tensor_scalar(sc8[u].rearrange("p (j c) -> p c j", j=2),
                                                        ss[w][:, 0:8].rearrange("p (c j) -> p c j", j=2), 8.0, None, ALU.mult))

        def qkT(k):
            s, kb, u = B[k], k % 8, k % 2
            for i in range(2):
                own(2 + i)
                pe.need(s["kn"] if i else s["rot"])
                for c in range(4):
                    t = pe.do(lambda e, i=i, c=c: e.transpose(bank(2 + i)[:, c * P:(c + 1) * P],
                                                              qr[u][:, i * 512 + c * P:i * 512 + (c + 1) * P], identF[:]), c == 3)
                act.need(t, at(k - 2, "sc"))
                dst = KT[:, :, kb * P:(kb + 1) * P] if i else QT[u]
                a = act.do(lambda e, i=i, dst=dst: e.copy(dst, bank(2 + i).rearrange("p (c n) -> p c n", c=4)))
                free(2 + i, a)
            s["tqk"], s["qkT"] = t, a

        sv = bank(4, 4).rearrange("p (b q) -> p b q", b=4)

        def scores(k):
            s, kb, u = B[k], k % 8, k % 2
            lo = 0 if kb else DH
            s["lo"] = lo
            pe.need(s["qkT"], m_bandB)
            for b in range(4):
                own(4 + b)
                j = b // 2
                rows = slice(64 * j, 64 * j + 64)
                for q in range(2):
                    hp = 2 * (b % 2) + q
                    o = W3 * q
                    pe.do(lambda e, b=b, o=o, rows=rows, hp=hp: e.matmul(
                        bank(4 + b)[:, o + lo:o + W3], QT[u][rows, hp, :], KT[rows, hp, kb * P - DH + lo:kb * P + P],
                        start=True, stop=False), False)
                    t = pe.do(lambda e, b=b, o=o: e.matmul(bank(4 + b)[:, o + lo:o + W3], identB[:], band[:, DH + lo:256],
                                                           start=False, stop=True), q == 1)
                dve.need(t, at(k - 2, "exp"))
                pb = bank(4 + b)[:, 0:2 * W3].rearrange("p (q n) -> p q n", q=2)
                d = dve.do(lambda e, b=b, pb=pb: e.tensor_reduce(nmx[u][:, 2 * b:2 * b + 2], pb[:, :, lo:W3], AX.X, ALU.max,
                                                                 negate=True))
                dve.need(d)
                d = dve.do(lambda e, b=b: e.tensor_tensor(nmx[u][:, 2 * b:2 * b + 2], nmx[u][:, 2 * b:2 * b + 2],
                                                          sc8[u][:, 2 * b:2 * b + 2], ALU.mult))
                act.need(d, at(k - 1, "te"), at(k - 2, "rz"))
                for q in range(2):
                    a = act.do(lambda e, b=b, q=q, pb=pb: e.activation(
                        E[:, 2 * b + q, lo:W3], pb[:, q, lo:W3], ACT.Exp, bias=nmx[u][:, 2 * b + q:2 * b + q + 1],
                        scale=sc8[u][:, 2 * b + q:2 * b + q + 1], accum_out=Z[u][:, 2 * b + q:2 * b + q + 1]))
                free(4 + b, a)
                s["exp%d" % b] = a
            s["sc"], s["exp"] = t, a
            dve.need(a, at(k - 2, "o"))
            s["rz"] = dve.do(lambda e: e.reciprocal(rZ[u], Z[u]))

        def eT(k):
            s = B[k]
            lo = s["lo"]
            for b in range(4):
                own(4 + b)
                pe.need(s["exp%d" % b])
                for q in range(2):
                    t = pe.do(lambda e, b=b, q=q: e.transpose(bank(4 + b)[:, 256 * q + P:256 * q + 256], E[:, 2 * b + q, DH:W3],
                                                              identF[:]), q == 1)
                if lo == 0:
                    for q in range(2):
                        t = pe.do(lambda e, b=b, q=q: e.transpose(bank(4 + b)[0:DH, 256 * q:256 * q + P], E[:, 2 * b + q, 0:DH],
                                                                  identF[:]), q == 1)
                pb = bank(4 + b).rearrange("p (q n) -> p q n", q=2)
                q, cp = (act, "copy") if b % 2 else (dve, "tensor_copy")
                q.need(t, at(k - 1, "av"))
                fn = (lambda e, o, i: e.copy(o, i)) if b % 2 else (lambda e, o, i: e.tensor_copy(o, i))
                a = q.do(lambda e, b=b, pb=pb, fn=fn: fn(e, ET[:, 2 * b:2 * b + 2, P:256], pb[:, :, P:256]))
                if lo == 0:
                    a = q.do(lambda e, b=b, pb=pb, fn=fn: fn(e, ET[0:DH, 2 * b:2 * b + 2, 0:P], pb[0:DH, :, 0:P]))
                free(4 + b, a)
                s["eT%d" % b] = a
            s["te"] = t

        def av(k):
            s, kb, u = B[k], k % 8, k % 2
            own(3)
            pe.need(s["v"], *(s["eT%d" % b] for b in range(4)))
            for n in range(8):
                h = 2 * (n % 4) + n // 4
                dst = bank(3)[:, n * DH:(n + 1) * DH]
                t = pe.do(lambda e, n=n, h=h, dst=dst: e.matmul(dst, ET[:, n, P:256], V[:, kb, h * DH:(h + 1) * DH],
                                                                start=True, stop=(s["lo"] > 0)), n == 7)
                if s["lo"] == 0:
                    t = pe.do(lambda e, n=n, h=h, dst=dst: e.matmul(dst, ET[0:DH, n, 0:P], VP[0:DH, kb - 1, h * DH:(h + 1) * DH],
                                                                    start=False, stop=True), n == 7)
            s["av"] = t
            dve.need(t, s["rz"], at(k - 1, "to"))
            s["o"] = dve.do(lambda e: e.tensor_tensor(O.rearrange("p (c j d) -> p j c d", c=4, j=2),
                                                      bank(3).rearrange("p (j c d) -> p j c d", j=2, c=4),
                                                      rZ[u].rearrange("p (j c) -> p j c", j=2).unsqueeze(3).broadcast_to([P, 2, 4, DH]),
                                                      ALU.mult))
            free(3, s["o"])

        def out(k):
            s = B[k]
            pe.need(s["o"])
            own(3)
            for c in range(4):
                t = pe.do(lambda e, c=c: e.transpose(bank(3)[:, c * P:(c + 1) * P], O[:, c * P:(c + 1) * P], identF[:]), c == 3)
            s["to"] = t
            act.need(t, at(k - 1, "wo"))
            a = act.do(lambda e: e.copy(OT, bank(3)))
            free(3, a)
            return a

        def out2(k, a):
            s = B[k]
            pe.need(a)
            own(3)
            for c in range(4):
                t = pe.do(lambda e, c=c: e.matmul(bank(3)[:, 0:P], OT[:, c * P:(c + 1) * P], wo[:, c, :],
                                                  start=(c == 0), stop=(c == 3)), c == 3)
            s["wo"] = t
            dve.need(t, *mh[k // 8])
            d = dve.do(lambda e: e.tensor_tensor(X[:, k, :], X[:, k, :], bank(3)[:, 0:P], ALU.add))
            free(3, d)
            m_X[k] = d

        qkv(0)
        qkT(0)
        for k in range(17):
            if k < 16:
                scores(k)
            if k > 0:
                av(k - 1)
            if k + 1 < 16:
                qkv(k + 1)
            if k > 0:
                a = out(k - 1)
            if k < 16:
                eT(k)
            if k > 0:
                out2(k - 1, a)
            if k + 1 < 16:
                qkT(k + 1)
        last = {"rot": B[15]["rot"]}
        for k in range(16):
            for key, m in B[k].items():
                last[(key, k - 16)] = m

        dve.need(*m_w)
        mhs = [shifted(b, m_X[8 * b + 7], [t_h]) for b in range(NB)]
        mn = []
        for b in range(NB):
            dve.need(mhs[b][1])
            m = layernorm(H, H, lambda k, b=b: mhs[b][0], ks=range(8 * b, 8 * b + 8))
            mn.append([m[8 * b + 7]])
        act.need(*m_w2)
        t_h, m_HT = transposed(mn, [B[15]["HT"]], True)
        dve.need(t_h)
        zero_rows = [dve.do(lambda e, b=b: e.memset(H[0:1, 8 * b, 64:128], 0.0)) for b in range(NB)]
        for b in range(NB):
            ks = slice(8 * b, 8 * b + 8)
            dve.need(*mhs[0], *mhs[1])
            d = dve.do(lambda e, ks=ks: e.tensor_tensor(X[:, ks, :], X[:, ks, :], b2.unsqueeze(1).broadcast_to([P, 8, DM]), ALU.add))
        dve.need(d)
        C = [dict() for _ in range(16)]

        def atc(k, key):
            return C[k].get(key) if k >= 0 else last.get((key, k))

        def up(k):
            s, u = C[k], k % 2
            pe.need(m_HT[k], *m_w2)
            b0 = 2 * u
            for c in (1, 0):
                own(b0 + c)
                s["w1%d" % c] = pe.do(lambda e, c=c: e.matmul(bank(b0 + c)[:, 0:HID], HT[:, k * P:(k + 1) * P],
                                                              w1[:, c * HID:(c + 1) * HID], start=True, stop=True))
            dve.need(s["w11"], atc(k - 2, "tp"))
            d1 = dve.do(lambda e: e.tensor_tensor(G[u], bank(b0 + 1)[:, 0:HID], b1[:, HID:2 * HID], ALU.add))
            free(b0 + 1, d1)
            dve.need(s["w10"])
            d2 = dve.do(lambda e: e.tensor_tensor(A[u], bank(b0)[:, 0:HID], b1[:, 0:HID], ALU.add))
            free(b0, d2)
            act.need(d1)
            a = act.do(lambda e: e.activation(G[u], G[u], ACT.Gelu))
            s["ge"] = (a, d2)

        def mid(k):
            s, u = C[k], k % 2
            dve.need(*s["ge"])
            d = dve.do(lambda e: e.tensor_tensor(G[u], G[u], A[u], ALU.mult))
            pe.need(d)
            bk = 4 + u
            own(bk)
            for c in range(3):
                n = min(P, HID - c * P)
                t = pe.do(lambda e, c=c, n=n: e.transpose(bank(bk)[0:n, c * P:(c + 1) * P], G[u][:, c * P:c * P + n], identF[:]),
                          c == 2)
            s["tp"] = t
            act.need(t, atc(k - 2, "w2"))
            act.do(lambda e: e.copy(PT[u][:, 0:2, :], bank(bk)[:, 0:256].rearrange("p (c n) -> p c n", c=2)), False)
            a = act.do(lambda e: e.copy(PT[u][0:85, 2, :], bank(bk)[0:85, 256:384]))
            free(bk, a)
            s["pt"] = a

        def down(k):
            s, u = C[k], k % 2
            bk = 6 + u
            pe.need(s["pt"])
            own(bk)
            for c in range(3):
                n = min(P, HID - c * P)
                t = pe.do(lambda e, c=c, n=n: e.matmul(bank(bk)[:, 0:P], PT[u][0:n, c, :], w2[0:n, c, :],
                                                       start=(c == 0), stop=(c == 2)), c == 2)
            s["w2"] = t
            dve.need(t)
            m_X[k] = dve.do(lambda e: e.tensor_tensor(X[:, k, :], X[:, k, :], bank(bk)[:, 0:P], ALU.add))
            free(bk, m_X[k])

        for k in range(18):
            if k < 16:
                up(k)
            if 0 <= k - 1 < 16:
                mid(k - 1)
            if 0 <= k - 2 < 16:
                down(k - 2)
        for k in range(16):
            for key, m in C[k].items():
                last[(key, k - 16)] = m
        htfree = [C[15]["w10"]]
        rel = [m_X[15], C[15]["w2"]]
    m = layernorm(X, X, lambda k: m_X[k])
    dve.need(m[15])
    s_out = sem("s_out")
    for b in range(NB):
        ks = slice(8 * b, 8 * b + 8)
        d = dve.do(lambda e, ks=ks: e.tensor_tensor(x0[:, ks, :], x0[:, ks, :], X[:, ks, :], ALU.add))
        sp.need(d)
        sp.dma(lambda e, b=b, ks=ks: e.dma_start(OUT[b].rearrange("(k p) d -> p k d", p=P), x0[:, ks, :]), s_out, 16)
    sp.ops.append((s_out, 32))


def constants():
    i = np.arange(P)
    causal = np.zeros((2, P, P), np.float32)
    causal[0] = np.where(i[None, :] <= i[:, None], 0.0, -BIG)
    causal[1] = causal[0].T
    j = np.arange(2 * P) - P
    diff = i[:, None] - j[None, :]
    band = np.where((diff >= 0) & (diff <= 64), 0.0, -BIG).astype(np.float32)
    f = np.float32
    hidx = np.arange(0, DH, 2, dtype=f)
    inv = (f(1.0) / np.power(f(10000.0), hidx / f(DH))).astype(f)
    t = np.arange(NT, dtype=f)
    fr = (t[:, None] * inv[None, :]).astype(f)
    fr = np.concatenate([fr, fr], -1).astype(np.float64)
    base = ((hidx + f(0.4 * DH)) / f(1.4 * DH)).astype(f)
    power = ((t - NT // 2) / f(32.0)).astype(f)
    sc = base[None, :].astype(np.float64) ** power[:, None].astype(np.float64)
    sc = np.concatenate([sc, sc], -1)
    sign = np.concatenate([-np.ones(DH // 2), np.ones(DH // 2)])
    cos, sin = np.cos(fr), np.sin(fr) * sign
    rot = np.stack([np.stack([cos * sc, cos / sc], 1), np.stack([sin * sc, sin / sc], 1)]).astype(f)
    return {"c_ident": np.eye(P, dtype=f), "c_causal": causal, "c_band": band, "c_rot": rot}


def kernel(**inputs):
    import concourse.bacc as bacc
    from concourse.bass_utils import run_bass_kernel_spmd

    nc = bacc.Bacc("TRN2", target_bir_lowering=False, num_devices=1)
    arrays = {k: np.ascontiguousarray(v) for k, v in inputs.items()}
    arrays.update(constants())
    I = {k: nc.dram_tensor("in_" + k, a.shape, mybir.dt.from_np(a.dtype), kind="ExternalInput").ap() for k, a in arrays.items()}
    out = nc.dram_tensor("out_0", (NB, NT, DM), F32, kind="ExternalOutput").ap()
    program(nc, I, out)
    r = run_bass_kernel_spmd(nc, [{"in_" + k: a for k, a in arrays.items()}], core_ids=[0])
    return r.results[0]["out_0"]
```

```python
from contextlib import ExitStack

import numpy as np

import concourse.bass as bass
from concourse import mybir

F32 = mybir.dt.float32
F32R = mybir.dt.float32r
BF16 = mybir.dt.bfloat16
ACT = mybir.ActivationFunctionType
ALU = mybir.AluOpType
AX = mybir.AxisListType

P = 128
NB, NT, DM = 2, 1024, 128
NBLK = NT // P
HA, DH = 16, 64
HB = 8
INNER = HB * DH
HID = 341
DEPTH = 2
EPS = 1e-5
BIG = float(2.0 ** 100)


class Eng:

    def __init__(self, sem):
        self.sem, self.n, self.ops, self.seen = sem, 0, [], {}

    def need(self, *marks):
        for m in marks:
            if m is not None and self.seen.get(id(m[0]), 0) < m[1]:
                self.seen[id(m[0])] = m[1]
                self.ops.append((m[0], m[1]))

    def do(self, fn, sig=True):
        if sig:
            self.n += 1
        self.ops.append((fn, sig))
        return (self.sem, self.n) if sig else None

    def dma(self, fn, sem, count):
        self.ops.append((fn, sem, count))

    def emit(self, eng):
        for op in self.ops:
            if len(op) == 3:
                op[0](eng).then_inc(op[1], 16)
            elif callable(op[0]):
                ins = op[0](eng)
                if op[1]:
                    ins.then_inc(self.sem, 1)
            else:
                eng.wait_ge(op[0], op[1])


def program(nc, I, OUT):
    with ExitStack() as ctx:
        cnt = [0]
        scope = [ctx]

        def sb(shape, dt=F32):
            cnt[0] += 1
            return scope[0].enter_context(nc.sbuf_tensor(f"t{cnt[0]}", shape, dt))

        def ar(n):
            return sb([P, n])[:, :]

        def sem(name):
            return ctx.enter_context(nc.semaphore(name))

        pe, dve, act, pool, sp = (Eng(sem("s_" + n)) for n in ("pe", "dve", "act", "pool", "sp"))
        PS = ctx.enter_context(nc.psum_tensor("PS", [P, 8 * 512], F32))
        bank_free = [[] for _ in range(8)]

        def bank(k, n=1):
            return PS[:, k * 512:(k + n) * 512]

        def own(k, n=1):
            for b in range(k, k + n):
                pe.need(*bank_free[b])

        def free(k, *marks):
            bank_free[k] = list(marks)

        nload = [0]

        def load(dst, src, after=()):
            s = sem(f"ld{nload[0]}")
            nload[0] += 1
            sp.need(*after)
            sp.dma(lambda e: e.dma_start(dst, src), s, 16)
            return (s, 16)

        x0 = sb([P, 16, DM])
        x_tiles = I["L0_attn_x"].rearrange("b (k p) d -> p (b k) d", p=P)
        m_x = [load(x0[:, 4 * g:4 * g + 4, :], x_tiles[:, 4 * g:4 * g + 4, :]) for g in range(2)]
        identF = sb([P, P])
        gam_in = sb([P, 1])
        cm = sb([P, 2, P])
        m_id = load(identF[:], I["c_ident"])
        identR = sb([P, P], F32R)
        identB = sb([P, P], BF16)
        half = sb([P, 16])
        fsc = sb([P, 3])
        st6 = sb([P, 16, 6])
        mv = sb([P, 16, 2])
        rs = sb([P, 16])
        X = sb([P, 16, DM])
        gam_out = sb([P, DM])
        wqkv0 = ar(1536)
        first = ExitStack()
        scope[0] = first
        WqD = ar(1024).rearrange("p (h d) -> p h d", h=HA)
        WkD = ar(1024).rearrange("p (h d) -> p h d", h=HA)
        m_wq = [load(WqD, I["L0_attn_Wq"].rearrange("f (h d) -> f h d", h=HA))]
        m_wk = [load(WkD, I["L0_attn_Wk"].rearrange("f (h d) -> f h d", h=HA))]
        m_gin = load(gam_in[:], I["L0_attn_gamma_in"].rearrange("(d a) -> d a", a=1))
        WV2 = ar(2048).rearrange("p (h d) -> p h d", h=HA)
        OF = [ar(1024).rearrange("p (k d) -> p k d", k=8) for _ in range(2)]
        Wv = OF[0].rearrange("p k d -> p (k d)")
        m_wv = load(Wv[:], I["L0_attn_Wv"])
        w0d = sb([P, P])
        m_z0 = dve.do(lambda e: e.memset(w0d[:], 0.0))
        m_w0d = [load(w0d[t * DH:(t + 1) * DH, t * DH:(t + 1) * DH], I["L0_attn_gnn_w"][0], after=[m_z0]) for t in range(2)]
        m_wv2 = load(WV2[:, :, 0:DH], I["L0_attn_Wv"].rearrange("f (h d) -> f h d", h=HA))
        m_cm = load(cm[:], I["c_causal"].rearrange("a p d -> p a d"))
        WG = sb([66, 130])
        m_wgz = dve.do(lambda e: e.memset(WG[:], 0.0))
        m_wg = [load(WG[:, 0:DH], I["c_ident"][0:66, 0:DH], after=[m_wgz]), load(WG[0:DH, DH:P], I["L0_attn_gnn_w"][0]),
                load(WG[:, P:130], I["c_ident"][0:66, 64:66])]
        WW1 = sb([P, DH])
        m_ww1 = [load(WW1[t * DH:(t + 1) * DH, :], I["L0_attn_gnn_w"][1]) for t in range(2)]
        WO = ar(2048).rearrange("p (h d) -> p h d", h=HA)
        m_wo = load(WO[0:DH, :, :], I["L0_attn_Wo"].rearrange("(h e) n -> e h n", h=HA))
        linw = sb([DH, DH])
        m_lw = load(linw[:], I["L0_attn_lin_w"])
        linb = sb([DH, 1])
        m_lb = load(linb[:], I["L0_attn_lin_b"].rearrange("(d a) -> d a", a=1))
        gb = sb([P, 2, DH])
        m_gb = [load(gb[:, t, :], I["L0_attn_gnn_b"][t:t + 1, :].broadcast_to([P, DH])) for t in range(2)]
        m_wqkv0 = load(wqkv0, I["L0_ffn_wqkv"][0])
        m_gout = load(gam_out[:], I["L0_attn_gamma_out"].rearrange("(a d) -> a d", a=1).broadcast_to([P, DM]))

        m_x += 2 * [load(x0[:, 8:16, :], x_tiles[:, 8:16, :])]

        cmB = sb([P, 2, P], BF16)
        m_half = pool.do(lambda e: e.memset(half[:], -0.5))

        def layernorm(dst, src, m_src, ks=range(16), gam=None, m_gam=None, twice=False):
            ks = list(ks)
            a, z = ks[0], ks[-1] + 1
            for k in ks:
                dve.need(m_src(k))
                m = dve.do(lambda e, k=k: e.bn_stats(st6[:, k, :], src[:, k, :]))
            dve.need(m)
            for k in ks:
                m = dve.do(lambda e, k=k: e.bn_aggr(mv[:, k, :], st6[:, k, :]))
            dve.need(m)
            m = dve.do(lambda e: e.tensor_scalar(rs[:, a:z], mv[:, a:z, 1], 1.0 + EPS if twice else 1.0,
                                                 EPS * EPS if twice else EPS, ALU.mult, ALU.add))
            pool.need(m, m_half)
            m = pool.do(lambda e: e.tensor_tensor(rs[:, a:z], rs[:, a:z], half[:, a:z], ALU.pow))
            dve.need(m, m_gam)
            out = {}
            for k in ks:
                out[k] = dve.do(lambda e, k=k: e.tensor_scalar(dst[:, k, :], src[:, k, :], mv[:, k, 0:1], rs[:, k:k + 1],
                                                               ALU.subtract, ALU.mult))
            if gam is not None:
                dve.need(out[ks[-1]])
                m = dve.do(lambda e: e.tensor_tensor(dst[:, a:z, :], dst[:, a:z, :],
                                                     gam[:].unsqueeze(1).broadcast_to([P, z - a, DM]), ALU.mult))
                out = {k: m for k in ks}
            return out

        ini = sb([P, 2, 66])
        m_i0 = dve.do(lambda e: e.memset(ini[:, 0, :], 0.0))
        m_i1 = dve.do(lambda e: e.memset(ini[:, 1, :], 1.0))
        dve.need(m_i0, m_i1)
        R3 = 2
        K2 = [sb([66, NT], F32R) for _ in range(R3)]
        VH = [sb([P, 8, 66], F32R) for _ in range(R3)]
        VL = [sb([P, 8, 66], F32R) for _ in range(R3)]
        NM = sb([P, 8, 66], F32R)
        for i in range(R3):
            dve.do(lambda e, i=i: e.tensor_copy(VL[i][:, :, 64:66], ini[:, 0:1, 0:2].broadcast_to([P, 8, 2])))
            dve.do(lambda e, i=i: e.tensor_copy(VH[i][:, :, 64:66], ini[:, 1:2, 0:2].broadcast_to([P, 8, 2])))
            dve.do(lambda e, i=i: e.tensor_copy(K2[i][64:66, :], ini[64:66, 1, 0:1].broadcast_to([2, NT])))
        m_ini = dve.do(lambda e: e.tensor_copy(NM[:, :, 0:64], ini[:, 0:1, 0:64].broadcast_to([P, 8, 64])))
        LW = sb([DH, P])
        LBc = sb([DH, P])
        ylin = sb([P, P])
        m_lz = dve.do(lambda e: e.memset(LW[:], 0.0))

        xn = Y = X
        xh, xl = sb([P, 2048], F32R), sb([P, 2048], F32R)
        m_xn, m_xnT, m_Y = {}, {}, {}

        def normed(k0, n):
            m = layernorm(xn, x0, lambda k: m_x[k0 // 4], ks=range(k0, k0 + n), twice=True)
            for k in range(k0, k0 + n):
                m_xn[k] = m[k]

        def turned(g, bk):
            own(bk)
            pe.need(m_id, *(m_xn[4 * g + r] for r in range(4)))
            for r in range(4):
                t = pe.do(lambda e, r=r: e.transpose(bank(bk)[:, r * P:(r + 1) * P], xn[:, 4 * g + r, :], identF[:]), r == 3)
            sl = slice(g * 512, (g + 1) * 512)
            act.need(t, m_gin)
            a = act.do(lambda e: e.activation(xh[:, sl], bank(bk), ACT.Copy, scale=gam_in[:, 0:1]))
            dve.need(a, m_gin)
            m_xnT[g] = dve.do(lambda e: e.scalar_tensor_tensor(xl[:, sl], bank(bk), gam_in[:, 0:1], xh[:, sl].bitcast(F32),
                                                               ALU.mult, ALU.subtract))
            free(bk, m_xnT[g])

        normed(0, 4)
        normed(4, 4)
        turned(0, 0)
        turned(1, 1)
        dve.need(m_id, m_cm)
        m_idR = dve.do(lambda e: e.tensor_copy(identR[:], identF[:]))
        dve.do(lambda e: e.tensor_copy(identB[:], identF[:]))
        m_cmB = dve.do(lambda e: e.tensor_copy(cmB[:], cm[:]))

        m_wv2p = []

        def values():
            WvT = xn[:, 8:16, :].rearrange("p k d -> p (k d)")
            for g in range(2):
                own(4 + g)
                pe.need(m_wv, m_id)
                for r in range(4):
                    t = pe.do(lambda e, g=g, r=r: e.transpose(bank(4 + g)[:, r * P:(r + 1) * P],
                                                              Wv[:, (4 * g + r) * P:(4 * g + r + 1) * P], identF[:]), r == 3)
                act.need(t)
                m_wvT = act.do(lambda e, g=g: e.copy(WvT[:, g * 512:(g + 1) * 512], bank(4 + g)))
                free(4 + g, m_wvT)
            pe.need(m_wvT, *m_w0d)
            for g in range(2):
                own(6 + g)
                for r in range(4):
                    t = pe.do(lambda e, g=g, r=r: e.matmul(bank(6 + g)[:, r * P:(r + 1) * P],
                                                           WvT[:, (4 * g + r) * P:(4 * g + r + 1) * P], w0d[:],
                                                           start=True, stop=True), r == 3)
                act.need(t)
                m_wv2p[:] = [act.do(lambda e, g=g: e.copy(WV2[:, 8 * g:8 * g + 8, DH:P],
                                                      bank(6 + g).rearrange("p (h d) -> p h d", h=8)))]
                free(6 + g, m_wv2p[0])

        m_WO = [None, None]

        def linear(g, bk):
            own(bk)
            if g == 0:
                pe.need(m_lw, m_id)
                t = pe.do(lambda e: e.transpose(bank(bk)[0:DH, 0:DH], linw[:], identF[0:DH, 0:DH]))
                dve.need(t, m_lb, m_lz)
                m = dve.do(lambda e: e.tensor_copy(LW[:, DH:P], bank(bk)[0:DH, 0:DH]))
                m_WO[1] = dve.do(lambda e: e.tensor_copy(LBc[:], linb[:].broadcast_to([DH, P])))
                free(bk, m)
            elif g < 5:
                pe.need(m_WO[1], m_wo)
                hs = slice(4 * g - 4, 4 * g)
                t = pe.do(lambda e: e.matmul(bank(bk), LW[:], WO[0:DH, hs, :], start=True, stop=True))
                act.need(t)
                m_WO[0] = act.do(lambda e: e.copy(WO[DH:P, hs, :], bank(bk)[DH:P].rearrange("p (h d) -> p h d", h=4)))
                free(bk, m_WO[0])
            else:
                for h in range(HA):
                    t = pe.do(lambda e, h=h: e.matmul(bank(bk)[:, 0:P], LBc[:], WO[0:DH, h, :], start=(h == 0),
                                                      stop=(h == HA - 1)), h == HA - 1)
                dve.need(t)
                m = dve.do(lambda e: e.tensor_copy(ylin[:], bank(bk)[:, 0:P]))
                free(bk, m)
                dve.need(m)
                began(0)

        def began(b):
            dve.need(*(m_xnT[2 * b + g] for g in range(2)))
            m_Y[b] = dve.do(lambda e: e.tensor_copy(Y[:, 8 * b:8 * b + 8, :], ylin[:].unsqueeze(1).broadcast_to([P, 8, P])))

        Q1 = [sb([P, NT], F32R) for _ in range(R3)]
        K1 = [sb([P, NT], F32R) for _ in range(R3)]
        Q2 = [sb([66, NT], F32R) for _ in range(R3)]
        vB = [ar(512).rearrange("p (k d) -> p k d", k=8) for _ in range(R3)]
        vW = [ar(512).rearrange("p (k d) -> p k d", k=8) for _ in range(R3)]
        WD = [sb([P, 2, 2, P], F32R) for _ in range(2)]
        WR = [sb([P, 2, P], F32R) for _ in range(2)]
        nm = [sb([P, 2, 8]) for _ in range(2)]
        EC = 4608
        Eh = sb([P, EC], F32R)
        El = sb([P, EC], F32R)
        NS = 3
        Es = ar(NS * 512).rearrange("p (s n) -> p s n", s=NS)
        dscr = ar(128)
        eD = [sb([P, 8]) for _ in range(2)]
        RT = sb([66, NT])
        RT2 = ar(NT)
        gZ = [sb([P, 4, 8]) for _ in range(2)]
        t1 = ar(512).rearrange("p (k d) -> p k d", k=8)
        fF = [ar(512).rearrange("p (k d) -> p k d", k=8) for _ in range(2)]
        gf = ar(512).rearrange("p (k d) -> p k d", k=8)
        F2 = sb([P, 8, P], F32R)
        G2 = sb([P, 8, P], F32R)
        OFT = ar(1024)
        tiles = []
        off = 0
        for c in range(2):
            for jb in range(4 * c + 4):
                i0 = max(c * 512, jb * P)
                n = (c + 1) * 512 - i0
                tiles.append((c, jb, i0, n, off))
                off += n
        assert off == EC
        NH = NB * HA
        S = [dict() for _ in range(NH)]

        def f32(ap):
            return ap.bitcast(F32)

        def old(t, key):
            return S[t][key] if t >= 0 else None

        def widen(t):
            if t >= NH:
                return
            h = t % HA
            jobs = [(WD[t % 2][:, :, i, :].rearrange("p s (a d) -> p s a d", a=2), W[:, h:h + 1, :].broadcast_to([P, 2, DH]))
                    for i, W in enumerate((WkD, WqD))]
            pool.need(*m_wq, *m_wk, old(t - 2, "proj"))
            for part in (jobs, [(WR[t % 2], WV2[:, h, :])]):
                for T, W in part:
                    m = pool.do(lambda e, T=T, W=W: e.tensor_copy(T[:, 0], W))
                pool.need(m)
                for T, W in part:
                    m = pool.do(lambda e, T=T, W=W: e.tensor_tensor(T[:, 1], W, T[:, 0].bitcast(F32), ALU.subtract))
                if part is jobs:
                    S[t]["wd"] = m
                    pool.need(m_wv2, *m_wv2p, old(t - 2, "pv"))
                else:
                    S[t]["wr"] = m

        def proj(t, which, c, bk):
            if t >= NH:
                return
            b, h = divmod(t, HA)
            r, s = t % R3, S[t]
            i, T1, sc = (0, K1[r], 1.0) if which == "k" else (1, Q1[r], 0.125)
            sl = slice(c * 512, (c + 1) * 512)
            pe.need(m_xnT[2 * b + c], s["wd"])
            own(bk)
            for n, (w, x) in enumerate(((0, xh), (1, xh), (0, xl))):
                mm = pe.do(lambda e, n=n, w=w, x=x: e.matmul(bank(bk), WD[r][:, w, i, :], x[:, b * NT + c * 512:b * NT + (c + 1) * 512],
                                                             start=(n == 0), stop=(n == 2)), n == 2)
            s["proj"] = mm
            act.need(mm, old(t - R3, "sc"), old(t - R3, "smax_pe"), m_ini)
            mh = act.do(lambda e: e.activation(T1[:, sl], bank(bk), ACT.Copy, scale=sc))
            s["low", which, c] = (bk, mm, mh)
            s[which + "h"] = mh

        def lower(t, which, c):
            if t >= NH:
                return
            r, s = t % R3, S[t]
            bk, mm, mh = s["low", which, c]
            sl = slice(c * 512, (c + 1) * 512)
            dve.need(mm, mh, old(t - R3, "sc"))
            if which == "k":
                s["kl"] = dve.do(lambda e: e.tensor_tensor(K2[r][0:64, sl], bank(bk)[0:64, :], f32(K1[r][0:64, sl]), ALU.subtract))
                free(bk, s["kl"])
            else:
                s["ql"] = dve.do(lambda e: e.scalar_tensor_tensor(Q1[r][64:128, sl], bank(bk)[64:128, :], 0.125,
                                                                  f32(Q1[r][64:128, sl]), ALU.mult, ALU.subtract))
                free(bk, s["ql"])

        def upper(t, c):
            if t >= NH:
                return
            r, s = t % R3, S[t]
            sl = slice(c * 512, (c + 1) * 512)
            pool.need(s["qh"], old(t - R3, "sc"))
            s["q2"] = pool.do(lambda e: e.tensor_copy(Q2[r][0:64, sl], f32(Q1[r][0:64, sl])))

        def projv(t, c, bk):
            if t >= NH:
                return
            b, h = divmod(t, HA)
            r, s = t % R3, S[t]
            pe.need(m_xnT[2 * b + c], s["wr"])
            own(bk)
            for k in range(4):
                o = b * NT + (4 * c + k) * P
                for n, (w, x) in enumerate(((0, xh), (1, xh), (0, xl))):
                    mm = pe.do(lambda e, k=k, n=n, w=w, x=x, o=o: e.matmul(bank(bk)[:, k * P:(k + 1) * P], x[:, o:o + P],
                                                                           WR[r][:, w, :], start=(n == 0), stop=(n == 2)),
                               k == 3 and n == 2)
            s["pv"] = mm
            pv = bank(bk).rearrange("p (k d) -> p k d", k=4)
            ks = slice(4 * c, 4 * c + 4)
            act.need(mm, old(t - R3, ("n2", 1)), old(t - R3, "av"), m_ini)
            act.do(lambda e: e.copy(vW[r][:, ks, :], pv[:, :, DH:P]), False)
            a3 = act.do(lambda e: e.copy(VH[r][:, ks, 0:DH], pv[:, :, 0:DH]))
            dve.need(a3, *m_gb, old(t - R3, ("n6", 1)))
            s["vl"] = dve.do(lambda e: e.tensor_tensor(VL[r][:, ks, 0:DH], pv[:, :, 0:DH], f32(VH[r][:, ks, 0:DH]), ALU.subtract))
            s["vb"] = dve.do(lambda e: e.tensor_tensor(vB[r][:, ks, :], pv[:, :, 0:DH], gb[:, 0:1, :].broadcast_to([P, 4, DH]),
                                                       ALU.add))
            free(bk, s["vb"])
            s["va"] = a3

        UNITS = [(7, 0), (1, 0), (3, 0), (6, 1), (5, 0), (4, 0), (0, 0), (6, 0), (2, 0), (7, 1), (5, 1), (4, 1)]

        def smax(t, k):
            if t >= NH:
                return
            r, s = t % R3, S[t]
            ib, c = UNITS[k]
            pe.need(s["ql"], s["kh"], m_cmB)
            bk = k % 2
            own(bk)
            lo, hi = c * 512, min((ib + 1) * P, (c + 1) * 512)
            diag = c == ib // 4
            mm = pe.do(lambda e: e.matmul(bank(bk)[:, 0:hi - lo], Q1[r][:, ib * P:(ib + 1) * P], K1[r][:, lo:hi],
                                          start=True, stop=not diag), not diag)
            if diag:
                mm = pe.do(lambda e: e.matmul(bank(bk)[:, hi - lo - P:hi - lo], identB[:], cmB[:, 0, :], start=False, stop=True))
            dve.need(mm, old(t - 2, "nm"))
            md = dve.do(lambda e: e.tensor_reduce(nm[t % 2][:, c, ib:ib + 1], bank(bk)[:, 0:hi - lo], AX.X, ALU.max, negate=True))
            free(bk, md)
            s["smax_pe"] = mm
            s["units"] = s.get("units", 0) + 1
            if s["units"] < len(UNITS):
                return
            n = nm[t % 2]
            dve.need(md, old(t - 1, "mrow_pe"))
            m1 = dve.do(lambda e: e.tensor_tensor(n[:, 0, 4:8], n[:, 0, 4:8], n[:, 1, 4:8], ALU.min))
            dve.need(m1)
            m1 = dve.do(lambda e: e.tensor_copy(NM[:, :, 64], n[:, 0, :]))
            dve.need(m1)
            s["nm"] = dve.do(lambda e: e.tensor_tensor(NM[:, :, 65], n[:, 0, :], f32(NM[:, :, 64]), ALU.subtract))

        def mrow(t, c):
            if t >= NH:
                return
            r, s = t % R3, S[t]
            pe.need(s["nm"], m_idR)
            own(4)
            for k in range(4):
                mm = pe.do(lambda e, k=k: e.matmul(bank(4)[0:66, k * P:(k + 1) * P], NM[:, 4 * c + k, :], identR[:],
                                                   start=True, stop=True), k == 3)
            act.need(mm)
            s["q2m"] = act.do(lambda e: e.copy(Q2[r][64:66, c * 512:(c + 1) * 512], bank(4)[64:66, :]))
            free(4, s["q2m"])
            s["mrow_pe"] = mm

        est = [None] * NS
        enum = [0]

        def av(t, k):
            r, s = t % R3, S[t]
            c, jb, i0, n, o = tiles[k]
            if jb == 0:
                own(4)
            pe.need(s["E"][k], s["vl"], s["va"])
            dst = bank(4)[0:66, i0 - c * 512:512]
            pe.do(lambda e: e.matmul(dst, VH[r][:, jb, :], Eh[:, o:o + n], start=(jb == 0), stop=False), False)
            pe.do(lambda e: e.matmul(dst, VL[r][:, jb, :], Eh[:, o:o + n], start=False, stop=False), False)
            mm = pe.do(lambda e: e.matmul(dst, VH[r][:, jb, :], El[:, o:o + n], start=False, stop=(jb == 4 * c + 3)))
            if jb == 4 * c + 3:
                act.need(mm, old(t - 1, ("g0", c)))
                s["rt", c] = act.do(lambda e: e.copy(RT[:, c * 512:(c + 1) * 512], bank(4)[0:66, :]))
                free(4, s["rt", c])
            s["av"] = mm

        def scores(t, k):
            r, u, s = t % R3, t % 2, S[t]
            c, jb, i0, n, o = tiles[k]
            pe.need(s["q2m"], s["q2"], s["kl"], s["ql"])
            bk = 2 + k % 2
            own(bk)
            diag = jb >= 4 * c
            pe.do(lambda e: e.matmul(bank(bk)[:, 0:n], K1[r][:, jb * P:(jb + 1) * P], Q1[r][:, i0:i0 + n],
                                     start=True, stop=False), False)
            mm = pe.do(lambda e: e.matmul(bank(bk)[:, 0:n], K2[r][:, jb * P:(jb + 1) * P], Q2[r][:, i0:i0 + n],
                                          start=False, stop=not diag), not diag)
            if diag:
                mm = pe.do(lambda e: e.matmul(bank(bk)[:, 0:P], identB[:], cmB[:, 1, :], start=False, stop=True))
            q = enum[0] % NS
            enum[0] += 1
            act.need(mm, est[q], S[t - 1]["l2t"][k] if t else None)
            me = act.do(lambda e: e.activation(Es[:, q, 0:n], bank(bk)[:, 0:n], ACT.Exp))
            mh = act.do(lambda e: e.activation(Eh[:, o:o + n], bank(bk)[:, 0:n], ACT.Exp))
            free(bk, mh)
            dve.need(me)
            if diag:
                dve.need(old(t - 2, ("gz", 1)), s.get("e") or old(t - 1, "e"))
                s["e"] = dve.do(lambda e: e.scalar_tensor_tensor(
                    dscr[:, 0:P], Es[:, q, 0:P], 1.0, identF[:], ALU.mult, ALU.mult, accum_out=eD[u][:, jb:jb + 1]))
                s["e", c] = s["e"]
            dve.need(mh)
            est[q] = dve.do(lambda e: e.tensor_tensor(El[:, o:o + n], Es[:, q, 0:n], f32(Eh[:, o:o + n]), ALU.subtract))
            s.setdefault("E", {})[k] = est[q]
            s["sc"] = mm

        est = [None] * NS
        enum = [0]

        def bc(ap):
            return ap.unsqueeze(2).broadcast_to([P, 8, DH])

        def graph1(t, c, b0):
            r, u, s = t % R3, t % 2, S[t]
            pe.need(s["rt", c], *m_wg)
            own(b0, 2)
            for k in range(4):
                mm = pe.do(lambda e, k=k: e.matmul(bank(b0 + k // 2)[:, 130 * (k % 2):130 * (k % 2) + 130],
                                                   RT[0:66, (4 * c + k) * P:(4 * c + k + 1) * P], WG[:],
                                                   start=True, stop=True), k == 3)
            s["g0", c] = mm
            ks = slice(4 * c, 4 * c + 4)
            pv = bank(b0, 2).rearrange("p (b x) -> p b x", b=2)[:, :, 0:260].rearrange("p b (k d) -> p b k d", k=2)
            g = gZ[u]

            def four(ap):
                return ap.rearrange("p (b k) d -> p b k d", b=2)

            def col(i):
                return four(g[:, i, ks].unsqueeze(2).broadcast_to([P, 4, DH]))

            dve.need(mm, s["e", c], old(t - 2, "p1"))
            z, ed = pv[:, :, :, 128], eD[u][:, ks].rearrange("p (b k) -> p b k", b=2)

            def two(i):
                return g[:, i, ks].rearrange("p (b k) -> p b k", b=2)

            a = dve.do(lambda e: e.tensor_tensor(two(1), z, ed, ALU.subtract))
            pool.need(a, s["va"], old(t - 1, ("n6", c)), old(t - 1, ("ge1", c)))
            n2 = pool.do(lambda e: e.tensor_tensor(t1[:, ks, :], vW[r][:, ks, :], g[:, 1, ks].unsqueeze(2).broadcast_to([P, 4, DH]),
                                                   ALU.mult))
            b_ = dve.do(lambda e: e.scalar_tensor_tensor(two(3), z, 2.0, ed, ALU.mult, ALU.subtract))
            c_ = dve.do(lambda e: e.reciprocal(two(2), z))
            dve.need(b_)
            d_ = dve.do(lambda e: e.reciprocal(g[:, 3, ks], g[:, 3, ks]))
            s["gz", c] = d_
            dve.need(n2)
            n3 = dve.do(lambda e: e.tensor_tensor(four(t1[:, ks, :]), four(t1[:, ks, :]), pv[:, :, :, DH:P], ALU.add))
            dve.need(n3, d_)
            n4 = dve.do(lambda e: e.tensor_tensor(t1[:, ks, :], t1[:, ks, :], g[:, 3, ks].unsqueeze(2).broadcast_to([P, 4, DH]),
                                                  ALU.mult))
            dve.need(n4, s["vb"])
            n6 = dve.do(lambda e: e.tensor_tensor(t1[:, ks, :], t1[:, ks, :], vB[r][:, ks, :], ALU.add))
            dve.need(c_, old(t - 2, "ofT"))
            n1 = dve.do(lambda e: e.tensor_tensor(four(OF[u][:, ks, 0:DH]), pv[:, :, :, 0:DH], col(2), ALU.mult))
            free(b0, n1)
            free(b0 + 1, n1)
            s["o1"] = n1
            s["n2", c], s["n6", c] = n2, n6

        def feats(t, c):
            if not 0 <= t < NH:
                return
            u, s = t % 2, S[t]
            ks = slice(4 * c, 4 * c + 4)
            used = S[t - 1]["l2t"][7 if c == 0 else 11] if t else None
            act.need(s["n6", c], old(t - 2, "p2"))
            s["ge1", c] = act.do(lambda e: e.activation(fF[u][:, ks, :], t1[:, ks, :], ACT.Gelu))
            act.need(s["ge1", c], used)
            a = act.do(lambda e: e.copy(F2[:, ks, 0:DH], fF[u][:, ks, :]))
            pool.need(s["ge1", c], old(t - 1, ("gl", c)))
            s["gf", c] = pool.do(lambda e: e.tensor_tensor(
                gf[:, ks, :], fF[u][:, ks, :], gZ[u][:, 1, ks].unsqueeze(2).broadcast_to([P, 4, DH]), ALU.mult))
            dve.need(a, used)
            s["f2", c] = dve.do(lambda e: e.tensor_tensor(F2[:, ks, DH:P], fF[u][:, ks, :], f32(F2[:, ks, 0:DH]), ALU.subtract))

        def share(t, c):
            if not 0 <= t < NH:
                return
            s = S[t]
            ks = slice(4 * c, 4 * c + 4)
            act.need(s["gf", c], old(t - 1, ("l2", c)))
            a2 = act.do(lambda e: e.copy(G2[:, ks, 0:DH], gf[:, ks, :]))
            dve.need(a2, s["gf", c])
            s["gl", c] = dve.do(lambda e: e.tensor_tensor(G2[:, ks, DH:P], gf[:, ks, :], f32(G2[:, ks, 0:DH]), ALU.subtract))

        def graph2(t, k):
            if not 0 <= t < NH:
                return
            s = S[t]
            c, jb, i0, n, o = tiles[k]
            pe.need(s["f2", jb // 4])
            if jb == 0:
                own(5)
            dst = bank(5)[:, i0 - c * 512:512]
            pe.do(lambda e: e.matmul(dst, F2[:, jb, :], Eh[:, o:o + n], start=(jb == 0), stop=False), False)
            s.setdefault("l2t", {})[k] = pe.do(lambda e: e.matmul(dst, F2[:, jb, :], El[:, o:o + n], start=False, stop=False))
            if jb == 4 * c + 3:
                pe.need(s["gl", c])
                for i in range(4):
                    mm = pe.do(lambda e, i=i: e.matmul(bank(5)[:, i * P:(i + 1) * P], G2[:, 4 * c + i, :], identR[:],
                                                       start=False, stop=(i == 3)), i == 3)
                act.need(mm, old(t - 1, "r2w"))
                s["rt2"] = act.do(lambda e: e.copy(RT2[:, c * 512:(c + 1) * 512], bank(5)))
                free(5, s["rt2"])
                s["l2", c] = mm

        def graph2b(t):
            u, s = t % 2, S[t]
            own(5)
            pe.need(s["rt2"], *m_ww1)
            for k in range(8):
                mm = pe.do(lambda e, k=k: e.matmul(bank(5)[:, k * DH:(k + 1) * DH], RT2[:, k * P:(k + 1) * P], WW1[:],
                                                   start=True, stop=True), k == 7)
            s["r2w"] = mm
            pool.need(s["gf", 0], s["gf", 1], s["f2", 0], s["f2", 1])
            fb = pool.do(lambda e: e.tensor_tensor(fF[u], fF[u], gb[:, 1:2, :].broadcast_to([P, 8, DH]), ALU.add))
            s["fuse"] = fb
            dve.need(mm, old(t - 1, "ge2"))
            p1 = dve.do(lambda e: e.tensor_tensor(t3, bank(5).rearrange("p (k d) -> p k d", k=8), bc(gZ[u][:, 3, :]), ALU.mult))
            free(5, p1)
            s["p1"] = p1
            pool.need(p1, fb)
            s["p2"] = pool.do(lambda e: e.tensor_tensor(t3, t3, fF[u], ALU.add))

        def gelu2(t):
            s = S[t]
            act.need(s["p2"], s["o1"])
            s["ge2"] = act.do(lambda e: e.activation(OF[t % 2][:, :, DH:P], t3, ACT.Gelu))

        def tailT(t, c):
            s, bk = S[t], 6 + c
            pe.need(s["ge2"], s["o1"])
            own(bk)
            for k in range(4):
                mm = pe.do(lambda e, k=k: e.transpose(bank(bk)[:, k * P:(k + 1) * P], OF[t % 2][:, 4 * c + k, :], identF[:]), k == 3)
            act.need(mm, old(t - 1, "y"))
            s["oft", c] = act.do(lambda e: e.copy(OFT[:, c * 512:(c + 1) * 512], bank(bk)))
            free(bk, s["oft", c])
            s["ofT"] = mm

        def tail(t, c):
            b, h = divmod(t, HA)
            s, bk = S[t], 6 + c
            pe.need(s["oft", c], m_WO[0])
            own(bk)
            for k in range(4):
                mm = pe.do(lambda e, k=k: e.matmul(bank(bk)[:, k * P:(k + 1) * P], OFT[:, (4 * c + k) * P:(4 * c + k + 1) * P],
                                                   WO[:, h, :], start=True, stop=True), k == 3)
            dve.need(mm, S[t - 1]["yd"] if h else m_Y[b])
            ks = slice(8 * b + 4 * c, 8 * b + 4 * c + 4)
            s["yd"] = dve.do(lambda e: e.tensor_tensor(Y[:, ks, :], Y[:, ks, :], bank(bk).rearrange("p (k d) -> p k d", k=4), ALU.add))
            free(bk, s["yd"])
            s["y"] = mm

        t3 = ar(512).rearrange("p (k d) -> p k d", k=8)
        LAG = 3
        NTL = len(tiles)
        values()
        widen(0)
        widen(1)
        for which, c, bk in (("q", 0, 2), ("k", 0, 3), ("q", 1, 4), ("k", 1, 5)):
            proj(0, which, c, bk)
            lower(0, which, c)
        upper(0, 0)
        upper(0, 1)
        for k in range(NTL):
            smax(0, k)
            if k in (1, 3):
                projv(0, k // 2, 6 + k // 2)
            if k in (5, 6, 7, 8):
                which, c = ("q", "k")[k % 2], (k - 5) // 2
                proj(1, which, c, k - 3)
                lower(1, which, c)
        upper(1, 0)
        upper(1, 1)
        widen(2)
        mrow(0, 0)
        mrow(0, 1)
        m_last, m_X = {}, {}

        def onward(k0, stage):
            ks = range(k0, k0 + 2)
            if stage == 0:
                m = layernorm(Y, Y, lambda k: S[16 * (k0 // 8) + 15]["yd"], ks=ks, gam=gam_out, m_gam=m_gout)
                m_last[k0] = m[k0 + 1]
            elif stage == 1:
                m = layernorm(Y, Y, lambda k: m_last[k0], ks=ks)
                dve.need(m[k0 + 1])
                m_last[k0] = dve.do(lambda e: e.tensor_tensor(x0[:, k0:k0 + 2, :], x0[:, k0:k0 + 2, :], Y[:, k0:k0 + 2, :], ALU.add))
            else:
                m = layernorm(Y, x0, lambda k: m_last[k0], ks=ks)
                for k in ks:
                    m_X[k] = m[k0 + 1]

        LEAD = 2
        def run(item, t):
            now, was, tl = t < NH, 0 <= t - 1 < NH, 0 <= t - 2
            name, k = item
            if name == "scores" and now:
                scores(t, k)
            elif name == "smax":
                smax(t + 1, k)
            elif name == "av" and now:
                av(t, k)
            elif name == "share0":
                share(t, 0)
            elif name == "share1":
                share(t - 1, 1)
            elif name == "upper" and t > 0:
                upper(t + 1, k)
            elif name == "feats":
                feats(t, k)
            elif name == "tailT" and tl:
                tailT(t - 2, k)
            elif name == "tail" and tl:
                tail(t - 2, k)
            elif name == "projv":
                projv(t + 1, k, 6 + k)
            elif name == "graph1" and now:
                graph1(t, k, 6)
            elif name == "graph2b" and was:
                graph2b(t - 1)
            elif name in ("projq", "projk"):
                proj(t + 2, name[4], k, (2 if name[4] == "q" else 0) + k)
            elif name in ("lowq", "lowk"):
                lower(t + 2, name[3], k)
            elif name == "mrow":
                mrow(t + 1, k)
            elif name == "gelu2" and was:
                gelu2(t - 1)
            elif name == "widen":
                widen(t + 3)
            elif name == "early":
                graph2(t, k)
            elif name == "late":
                graph2(t - 1, k)
            elif name == "once":
                if 18 <= t < 30 and k == 5:
                    onward(2 * ((t - 18) % 4), (t - 18) // 4)
                if t == 0 and k in (1, 2, 3, 4, 8, 9):
                    linear((1, 2, 3, 4, 8, 9).index(k), 6 + k % 2)
                if 2 <= t < 6 and k == 5:
                    normed(4 + 2 * t, 2)
                if t in (6, 7) and k == 0:
                    turned(t - 4, 6)
                if t == 8 and k == 0:
                    began(1)

        SLOT = [('smax', 0), ('scores', 0), ('once', 0), ('scores', 1), ('smax', 1), ('tailT', 0), ('once', 1),
                ('share1', 0), ('late', 9), ('smax', 2), ('once', 2), ('tailT', 1), ('late', 6), ('scores', 2),
                ('scores', 3), ('upper', 0), ('smax', 3), ('once', 3), ('av', 0), ('tail', 0), ('tail', 1),
                ('scores', 4), ('smax', 4), ('once', 4), ('late', 8), ('scores', 5), ('smax', 5), ('once', 5),
                ('av', 1), ('upper', 1), ('scores', 6), ('late', 10), ('projv', 0), ('av', 2), ('smax', 6), ('av', 3),
                ('projv', 1), ('scores', 7), ('smax', 7), ('scores', 8), ('av', 4), ('late', 11), ('av', 5),
                ('once', 8), ('scores', 9), ('once', 9), ('smax', 8), ('scores', 10), ('smax', 9), ('graph1', 0),
                ('graph2b', 0), ('av', 6), ('scores', 11), ('av', 9), ('smax', 11), ('smax', 10), ('av', 7),
                ('feats', 0), ('projq', 0), ('av', 8), ('av', 10), ('lowq', 0), ('av', 11), ('projq', 1), ('projk', 0),
                ('lowq', 1), ('share0', 0), ('lowk', 0), ('gelu2', 0), ('mrow', 0), ('graph1', 1), ('projk', 1),
                ('early', 0), ('early', 2), ('mrow', 1), ('early', 1), ('lowk', 1), ('widen', 0), ('early', 3),
                ('early', 4), ('early', 5), ('early', 7), ('feats', 1)]
        for t in range(NH + 2):
            for item in SLOT:
                run(item, t)

        own(7)
        fence = (pe.do(lambda e: e.transpose(bank(7)[:, 0:P], identF[:], identF[:])), dve.do(lambda e: e.tensor_copy(fsc[:, 2:3], identF[:, 0:1])),
                 act.do(lambda e: e.copy(fsc[:, 0:1], identF[:, 0:1])), pool.do(lambda e: e.memset(fsc[:, 1:2], 0.0)))
        free(7, fence[0])
        for q in (pe, dve, act, pool, sp):
            q.need(*fence)
        first.close()
        scope[0] = ctx
        ffn(nc, I, ctx, locals())
        block = ctx.enter_context(nc.Block())
        block.sync(lambda e: sp.emit(e))
        block.tensor(lambda e: pe.emit(e))
        block.vector(lambda e: dve.emit(e))
        block.scalar(lambda e: act.emit(e))
        block.gpsimd(lambda e: pool.emit(e))


def ffn(nc, I, ctx, g):
    pe, dve, act, pool, sp = (g[n] for n in ("pe", "dve", "act", "pool", "sp"))
    X, x0, ar, load, bank, own, free, sb, layernorm = (g[n] for n in (
        "X", "x0", "ar", "load", "bank", "own", "free", "sb", "layernorm"))
    identF, identB, sem, half, fence, OUT = (g[n] for n in ("identF", "identB", "sem", "half", "fence", "OUT"))
    NA = DEPTH * 16
    NG = NA // 4
    QB, KB, VB, OB, SB, TB, FB = 0, 1, 2, 3, 4, 6, 7
    CH = [(c, min(P, HID - c * P)) for c in range(3)]

    def of(a):
        return a // 16, a % 16, a % 16 // 8, a % 8

    m_X, onward = g["m_X"], g["onward"]
    wqkv, wo, w1, w2, b1, lnp, qks, tabl = [], [], [], [], [], [], [], []
    tab = ar(4 * 512).rearrange("p (f k s d) -> p f k s d", f=2, k=8, s=2)
    for l in range(DEPTH):
        wqkv.append(ar(1536) if l else g["wqkv0"])
        wo.append(ar(512).rearrange("p (c n) -> p c n", c=4))
        w1.append(ar(2 * HID))
        w2.append(ar(384).rearrange("p (c n) -> p c n", c=3))
        b1.append(ar(6))
        lnp.append(ar(2))
        qks.append(ar(4 * DH).rearrange("p (f s d) -> p f s d", f=2, s=2))
        tabl.append(ar(4 * 512).rearrange("p (f k s d) -> p f k s d", f=2, k=8, s=2))
    HT = [ar(NT + 2) for _ in range(NB)]
    KT = [ar(4 * (NT + DH)).rearrange("p (c n) -> p c n", c=4) for _ in range(NB)]
    QT = [ar(512).rearrange("p (c n) -> p c n", c=4) for _ in range(2)]
    V = ar(8 * 512).rearrange("p (k n) -> p k n", k=8)
    VS = ar(8 * 512).rearrange("p (k n) -> p k n", k=8)
    qr = [ar(1024) for _ in range(2)]
    tm = ar(1024)
    sq = ar(1024)
    ss = [ar(16) for _ in range(3)]
    sc8 = [ar(8) for _ in range(3)]
    nmx = [ar(8) for _ in range(2)]
    Z = [ar(8) for _ in range(2)]
    rZ = [ar(8) for _ in range(2)]
    E = [ar(1024).rearrange("p (h n) -> p h n", h=8) for _ in range(2)]
    ET = [ar(1024).rearrange("p (h n) -> p h n", h=8) for _ in range(2)]
    OT = ar(512)
    H = ar(512).rearrange("p (k d) -> p k d", k=4)
    HF = ar(512)
    GP = ar(1536).rearrange("p (c n) -> p c n", c=3)
    PT = ar(1536).rearrange("p (c n) -> p c n", c=3)
    bandF = ar(256).rearrange("p (s n) -> p s n", s=2)
    band = sb([P, 2, P], BF16)
    shm = ar(256).rearrange("p (s n) -> p s n", s=2)

    m_z = [dve.do(lambda e, t=t: e.memset(t[64:P, 0:1], 0.0)) for t in HT]
    m_z += [dve.do(lambda e, t=t: e.memset(t[:, :, 0:DH], 0.0)) for t in KT]
    m_z.append(dve.do(lambda e: e.memset(VS[0:64, 0, :], 0.0)))
    m_z.append(dve.do(lambda e: e.memset(PT[64:P, 2, :], 1.0)))
    m_wqkv = [g["m_wqkv0"]]
    m_tab = [load(tab[:, f], I["c_rot"][f].rearrange("(k p) s d -> p k s d", p=P), after=fence) for f in range(2)]
    m_s, m_wo, m_w = [], [], []
    for l in range(DEPTH):
        m_s.append([])
        for s, name in enumerate(("L0_ffn_q_scale", "L0_ffn_k_scale")):
            src = I[name][l:l + 1, :]
            m_s[l] += [load(qks[l][:, 0, s, :], src.broadcast_to([P, DH])),
                       load(qks[l][:, 1, s, 0:32], src[:, 32:64].broadcast_to([P, 32])),
                       load(qks[l][:, 1, s, 32:64], src[:, 0:32].broadcast_to([P, 32]))]
        if l == 0:
            m_band = load(bandF, I["c_band"].rearrange("s p n -> p s n"))
            m_shm = load(shm, I["c_shift"].rearrange("s p n -> p s n"))
        else:
            m_wqkv.append(load(wqkv[l], I["L0_ffn_wqkv"][l]))
        m_wo.append(load(wo[l], I["L0_ffn_wo"][l].rearrange("(c p) n -> p c n", p=P)))
        w = [load(w1[l], I["L0_ffn_w1"][l]),
             load(w2[l][:, 0:2, :], I["L0_ffn_w2"][l][0:256, :].rearrange("(c p) n -> p c n", p=P)),
             load(w2[l][0:85, 2, :], I["L0_ffn_w2"][l][256:HID, :]),
             load(w2[l][85:86, 2, :], I["L0_ffn_b2"][l:l + 1, :]),
             load(lnp[l][:, 0:1], I["L0_ffn_ln_g"][l].rearrange("(d a) -> d a", a=1)),
             load(lnp[l][:, 1:2], I["L0_ffn_ln_b"][l].rearrange("(d a) -> d a", a=1))]
        for f in range(2):
            for c, n in CH:
                w.append(load(b1[l][0:n, 3 * f + c:3 * f + c + 1],
                              I["L0_ffn_b1"][l, f * HID + c * P:f * HID + c * P + n].rearrange("(d a) -> d a", a=1)))
        m_w.append(w)
    dve.need(m_band)
    m_bandB = dve.do(lambda e: e.tensor_copy(band[:], bandF))
    m_tabl = []

    def table(l, f, s):
        pool.need(*m_tab, *m_s[l], m_tabl[0] if l else None)
        m = pool.do(lambda e: e.tensor_tensor(tabl[l][:, f, :, s, :], tab[:, f, :, s, :],
                                              qks[l][:, f, s:s + 1, :].broadcast_to([P, 8, DH]), ALU.mult))
        if f and s:
            m_tabl.append(m)

    def later(n):
        if n < 4:
            table(1, n // 2, n % 2)


    B = [dict() for _ in range(NA)]
    F = [dict() for _ in range(NG)]
    s_vs = [sem(f"vs{i}") for i in range(4)]
    n_vs = [0] * 4

    def at(a, key):
        return B[a].get(key) if 0 <= a < NA else None

    def ft(q, key):
        return F[q].get(key) if 0 <= q < NG else None

    def xT(q):
        l, k0, b, kb = of(4 * q)
        own(FB)
        pe.need(*(m_X[k0 + r] for r in range(4)))
        for r in range(4):
            t = pe.do(lambda e, r=r: e.transpose(bank(FB)[:, r * P:(r + 1) * P], X[:, k0 + r, :], identF[:]), r == 3)
        act.need(t, *(at(4 * q - 16 + r, "qkv") for r in range(5)), *m_z)
        act.do(lambda e: e.copy(HT[b][0:64, kb * P:kb * P + 512], bank(FB)[0:64, :]))
        a = act.do(lambda e: e.copy(HT[b][64:P, kb * P + 1:kb * P + 513], bank(FB)[64:P, :]))
        free(FB, a)
        F[q]["xT"] = a
        F[q]["xr"] = t

    def qkv(a):
        s, (l, k, b, kb) = B[a], of(a)
        pe.need(F[a // 4]["xT"], m_wqkv[l])
        for c in range(3):
            own(QB + c)
            t = pe.do(lambda e, c=c: e.matmul(bank(QB + c), HT[b][:, kb * P:(kb + 1) * P], wqkv[l][:, c * 512:(c + 1) * 512],
                                              start=True, stop=True), c > 0)
            if c == 1:
                t1 = t
        s["qkv"] = t
        s["t1"], s["t2"] = t1, t

    def square(a):
        s = B[a]
        act.need(s["t1"], at(a - 1, "ss"))
        s["sq"] = act.do(lambda e: e.activation(sq, bank(QB, 2), ACT.Square))

    def values(a):
        s, (l, k, b, kb) = B[a], of(a)
        act.need(s["t2"], at(a - 8, "av"))
        s["v"] = act.do(lambda e: e.copy(V[:, kb, :], bank(VB)))
        free(VB, s["v"])
        i = a % 4
        sp.need(s["v"], at(a - 8, "av"), at(a - 7, "av"), m_z[-2], at(a - 3, "av"))
        sp.dma(lambda e: e.dma_start(VS[64:P, kb, :], V[0:64, kb, :]), s_vs[i], 16)
        n_vs[i] += 16
        if kb < 7:
            sp.dma(lambda e: e.dma_start(VS[0:64, kb + 1, :], V[64:P, kb, :]), s_vs[i], 16)
            n_vs[i] += 16
        s["vs"] = (s_vs[i], n_vs[i])

    def squares(a):
        s, w = B[a], a % 3
        m_sq = s["sq"]
        dve.need(m_sq, at(a - 3, "sc8"))
        d = dve.do(lambda e: e.tensor_reduce(ss[w], sq.rearrange("p (s d) -> p s d", d=DH), AX.X, ALU.add))
        s["ss"] = d
        dve.need(d)
        d = dve.do(lambda e: e.tensor_scalar(ss[w], ss[w], 1e-24, None, ALU.max))
        pool.need(d)
        s["pw"] = pool.do(lambda e: e.tensor_tensor(ss[w], ss[w], half[:], ALU.pow))

    def rotate(a):
        s, (l, k, b, kb), u = B[a], of(a), a % 2
        t1 = s["t1"]
        pv = bank(QB, 2).rearrange("p (s h d) -> p s h d", s=2, d=DH)
        r4 = qr[u].rearrange("p (s h d) -> p s h d", s=2, d=DH)
        t4 = tm.rearrange("p (s h d) -> p s h d", s=2, d=DH)
        dve.need(t1, m_tabl[l], at(a - 2, "tk"), at(a - 1, "rot"))
        dve.do(lambda e: e.tensor_tensor(r4, pv, tabl[l][:, 0, kb, :, :].unsqueeze(2).broadcast_to([P, 2, 8, DH]), ALU.mult))
        for hf in range(2):
            d = dve.do(lambda e, hf=hf: e.tensor_tensor(
                t4[:, :, :, 32 * hf:32 * hf + 32], pv[:, :, :, 32 - 32 * hf:64 - 32 * hf],
                tabl[l][:, 1, kb, :, 32 * hf:32 * hf + 32].unsqueeze(2).broadcast_to([P, 2, 8, 32]), ALU.mult))
        free(QB, d)
        free(KB, d)
        dve.need(d)
        s["rot"] = dve.do(lambda e: e.tensor_tensor(qr[u], qr[u], tm, ALU.add))

    def norms(a):
        s, u, w = B[a], a % 2, a % 3
        kr = qr[u][:, 512:1024].rearrange("p (h d) -> p h d", d=DH)
        dve.need(s["pw"], s["rot"], at(a - 3, "exp"))
        s["kn"] = dve.do(lambda e: e.tensor_tensor(kr, kr, ss[w][:, 8:16].unsqueeze(2).broadcast_to([P, 8, DH]), ALU.mult))
        s["sc8"] = dve.do(lambda e: e.tensor_scalar(sc8[w].rearrange("p (j c) -> p c j", j=2),
                                                    ss[w][:, 0:8].rearrange("p (c j) -> p c j", j=2), 8.0, None, ALU.mult))

    def qkT(a, i):
        s, (l, k, b, kb), u = B[a], of(a), a % 2
        own(TB)
        pe.need(s["kn"] if i else s["rot"])
        for c in range(4):
            t = pe.do(lambda e, c=c: e.transpose(bank(TB)[:, c * P:(c + 1) * P],
                                                 qr[u][:, i * 512 + c * P:i * 512 + (c + 1) * P], identF[:]), c == 3)
        act.need(t, at(a - 15, "sc") if i else at(a - 2, "sc"))
        dst = KT[b][:, :, DH + kb * P:DH + (kb + 1) * P] if i else QT[u]
        m = act.do(lambda e: e.copy(dst, bank(TB).rearrange("p (c n) -> p c n", c=4)))
        free(TB, m)
        s["tk" if i else "tq"] = t
        s["kT" if i else "qT"] = m

    def scores(a):
        s, (l, k, b, kb), u = B[a], of(a), a % 2
        pe.need(m_bandB, s["qT"], s["kT"], *m_z)
        s["sc_"] = []
        for j in range(2):
            own(SB + j)
            rows = slice(64 * j, 64 * j + 64)
            for c in range(4):
                for w in range(2):
                    pe.do(lambda e, j=j, c=c, w=w, rows=rows: e.matmul(
                        bank(SB + j)[64 * w:64 * w + 64, c * P:(c + 1) * P], QT[u][rows, c, 64 * w:64 * w + 64],
                        KT[b][rows, c, kb * P + 64 * w:kb * P + 64 * w + P], start=True, stop=False), False)
                t = pe.do(lambda e, j=j, c=c: e.matmul(bank(SB + j)[:, c * P:(c + 1) * P], identB[:], band[:, 0 if kb else 1, :],
                                                       start=False, stop=True), c == 3)
            s["sc_"].append(t)
        s["sc"] = t

    def softmax(a):
        s, u, w = B[a], a % 2, a % 3
        n4 = [slice(4 * j, 4 * j + 4) for j in range(2)]
        m_n = []
        for j in range(2):
            dve.need(s["sc_"][j], at(a - 2, "exp"))
            d = dve.do(lambda e, j=j: e.tensor_reduce(nmx[u][:, n4[j]], bank(SB + j).rearrange("p (c n) -> p c n", c=4), AX.X,
                                                      ALU.max, negate=True))
            dve.need(d, s["sc8"])
            m_n.append(dve.do(lambda e, j=j: e.tensor_tensor(nmx[u][:, n4[j]], nmx[u][:, n4[j]], sc8[w][:, n4[j]], ALU.mult)))
        s["mn"] = m_n

    def exps(a):
        s, u, w = B[a], a % 2, a % 3
        m_n = s["mn"]
        s["ex"] = []
        for j in range(2):
            act.need(m_n[j], at(a - 2, "te"), at(a - 2, "rz"))
            for c in range(4):
                n = 4 * j + c
                m = act.do(lambda e, j=j, c=c, n=n: e.activation(
                    E[u][:, n, :], bank(SB + j)[:, c * P:(c + 1) * P], ACT.Exp, bias=nmx[u][:, n:n + 1],
                    scale=sc8[w][:, n:n + 1], accum_out=Z[u][:, n:n + 1]), c == 3)
            free(SB + j, m)
            s["ex"].append(m)
        s["exp"] = m

    def normalise(a):
        s, u = B[a], a % 2
        s["en"] = []
        for j in range(2):
            n4 = slice(4 * j, 4 * j + 4)
            dve.need(s["ex"][j])
            d = dve.do(lambda e, n4=n4: e.reciprocal(rZ[u][:, n4], Z[u][:, n4]))
            dve.need(d)
            s["en"].append(dve.do(lambda e, n4=n4: e.tensor_tensor(
                E[u][:, n4, :], E[u][:, n4, :], rZ[u][:, n4].unsqueeze(2).broadcast_to([P, 4, P]), ALU.mult)))
        s["rz"] = s["en"][1]

    def eT(a):
        s, u = B[a], a % 2
        s["eT"] = []
        for j in range(2):
            own(SB + j)
            pe.need(s["en"][j])
            for c in range(4):
                t = pe.do(lambda e, j=j, c=c: e.transpose(bank(SB + j)[:, c * P:(c + 1) * P], E[u][:, 4 * j + c, :], identF[:]),
                          c == 3)
            act.need(t, at(a - 2, "av"))
            m = act.do(lambda e, j=j: e.copy(ET[u][:, 4 * j:4 * j + 4, :], bank(SB + j).rearrange("p (c n) -> p c n", c=4)))
            free(SB + j, m)
            s["eT"].append(m)
        s["te"] = t

    def av(a):
        s, (l, k, b, kb), u = B[a], of(a), a % 2
        own(OB)
        pe.need(s["vs"], at(a - 1, "vs") if kb else m_z[-2], s["v"], *s["eT"])
        for j in range(2):
            for c in range(4):
                h = 2 * c + j
                for w, v in enumerate((VS, V)):
                    t = pe.do(lambda e, j=j, c=c, h=h, w=w, v=v: e.matmul(
                        bank(OB)[64 * j:64 * j + 64, c * P + 64 * w:c * P + 64 * w + 64], v[:, kb, h * DH:(h + 1) * DH],
                        ET[u][:, 4 * j + c, 64 * w:64 * w + 64], start=True, stop=True), h == 7 and w == 1)
        s["av"] = t

    def outT(a):
        s = B[a]
        act.need(s["av"], at(a - 1, "wo"))
        s["oT"] = act.do(lambda e: e.copy(OT, bank(OB)))
        free(OB, s["oT"])

    def proj(a):
        s, (l, k, b, kb) = B[a], of(a)
        own(VB)
        pe.need(s["oT"], m_wo[l])
        for c in range(4):
            t = pe.do(lambda e, c=c: e.matmul(bank(VB)[:, 0:P], OT[:, c * P:(c + 1) * P], wo[l][:, c, :],
                                              start=(c == 0), stop=(c == 3)), c == 3)
        s["wo"] = t

    def add(a):
        s, (l, k, b, kb) = B[a], of(a)
        t = s["wo"]
        dve.need(t, m_X[k], F[a // 4]["xr"])
        m_X[k] = dve.do(lambda e: e.tensor_tensor(X[:, k, :], X[:, k, :], bank(VB)[:, 0:P], ALU.add))
        free(VB, m_X[k])

    def shift(q, FB=FB):
        s, (l, k0, b, kb) = F[q], of(4 * q)
        own(FB)
        pe.need(m_shm, *(m_X[k0 + r] for r in range(4)), m_X[k0 - 1] if kb else None)
        r0 = 0 if kb else 1
        pv = bank(FB)[:, 0:256].rearrange("p (r d) -> p r d", r=4)
        pe.do(lambda e: e.matmul(pv, shm[:, 0, :], X[:, k0:k0 + 4, 64:P], start=True, stop=False), False)
        t = pe.do(lambda e: e.matmul(pv[:, r0:4, :], shm[:, 1, :], X[:, k0 + r0 - 1:k0 + 3, 64:P], start=False, stop=True))
        s["sh"] = t
        act.need(t, ft(q - 1, "hT"))
        a = act.do(lambda e: e.copy(H[:, :, 64:P], pv))
        free(FB, a)
        pool.need(*(m_X[k0 + r] for r in range(4)), ft(q - 1, "hT"))
        p = pool.do(lambda e: e.tensor_copy(H[:, :, 0:64], X[:, k0:k0 + 4, 0:64]))
        dve.need(a, p)
        s["nrm"] = lambda: layernorm(H, H, lambda k: None, ks=range(4))[3]

    def hT(q, FB=FB):
        s, l = F[q], q // 4
        m = s["nrm"]()
        own(FB)
        pe.need(m)
        for r in range(4):
            t = pe.do(lambda e, r=r: e.transpose(bank(FB)[:, r * P:(r + 1) * P], H[:, r, :], identF[:]), r == 3)
        s["hT"] = t
        act.need(t, ft(q - 1, "up"), *m_w[l])
        s["hf"] = act.do(lambda e: e.activation(HF, bank(FB), ACT.Identity, bias=lnp[l][:, 1:2], scale=lnp[l][:, 0:1]))
        free(FB, s["hf"])

    def gate(q, c, FB=FB):
        s, l, n = F[q], q // 4, CH[c][1]
        own(FB)
        pe.need(s["hf"], *m_w[l])
        t = pe.do(lambda e: e.matmul(bank(FB)[0:n, :], w1[l][:, HID + c * P:HID + c * P + n], HF, start=True, stop=True))
        act.need(t, ft(q - 1, "pt"))
        m = act.do(lambda e: e.activation(GP[0:n, c, :], bank(FB)[0:n, :], ACT.Identity, bias=b1[l][0:n, 3 + c:4 + c]))
        free(FB, m)
        s["gt"] = s["gt%d" % c] = m

    def gelu(q):
        s, n = F[q], CH[2][1]
        act.need(s["gt"])
        act.do(lambda e: e.activation(GP[:, 0:2, :], GP[:, 0:2, :], ACT.Gelu))
        s["ge"] = act.do(lambda e: e.activation(GP[0:n, 2, :], GP[0:n, 2, :], ACT.Gelu))

    def up(q, c, FB=FB):
        s, l, n = F[q], q // 4, CH[c][1]
        own(FB)
        s["up"] = pe.do(lambda e: e.matmul(bank(FB)[0:n, :], w1[l][:, c * P:c * P + n], HF, start=True, stop=True))
        dve.need(s["up"], s["ge"], ft(q - 1, "dn"), *m_z, *m_w[l])
        s["pt"] = dve.do(lambda e: e.scalar_tensor_tensor(PT[0:n, c, :], bank(FB)[0:n, :], b1[l][0:n, c:c + 1], GP[0:n, c, :],
                                                          ALU.add, ALU.mult))
        free(FB, s["pt"])
        s["up%d" % c] = s["pt"]

    def down(q, FB=FB):
        s, (l, k0, b, kb) = F[q], of(4 * q)
        own(FB)
        pe.need(s["pt"], *m_w[l])
        for r in range(4):
            for c in range(3):
                n = (P, P, 86)[c]
                t = pe.do(lambda e, r=r, c=c, n=n: e.matmul(bank(FB)[:, r * P:(r + 1) * P], PT[0:n, c, r * P:(r + 1) * P],
                                                            w2[l][0:n, c, :], start=(c == 0), stop=(c == 2)), r == 3 and c == 2)
        s["dn"] = t
        dve.need(t, s["sh"], ft(q + 1, "sh"))
        m = dve.do(lambda e: e.tensor_tensor(X[:, k0:k0 + 4, :], X[:, k0:k0 + 4, :],
                                             bank(FB).rearrange("p (r d) -> p r d", r=4), ALU.add))
        free(FB, m)
        for r in range(4):
            m_X[k0 + r] = m

    s_out = sem("s_out")

    def finish(q):
        l, k0, b, kb = of(4 * q)
        ks = slice(k0, k0 + 4)
        m = layernorm(X, X, lambda k: m_X[k], ks=range(k0, k0 + 4))
        dve.need(m[k0 + 3])
        d = dve.do(lambda e: e.tensor_tensor(x0[:, ks, :], x0[:, ks, :], X[:, ks, :], ALU.add))
        sp.need(d)
        sp.dma(lambda e: e.dma_start(OUT[b].rearrange("(k p) d -> p k d", p=P)[:, kb:kb + 4, :], x0[:, ks, :]), s_out, 16)

    STEP = [('scores', 0), ('once', 0), ('softmax', 0), ('shift', 0), ('exps', 0), ('gate2', 2), ('norms', 0),
            ('norm', 0), ('qkv', 0), ('normalise', 0), ('hT', 1), ('square', 0), ('down', 4), ('gelu', 2),
            ('squares', 0), ('qkT', 0), ('up1', 3), ('rotate', 0), ('av', 0), ('outT', 0), ('gate1', 1), ('up0', 2),
            ('values', 0), ('eT', 0), ('qkT', 1), ('up2', 3), ('proj', 0), ('turn', 4), ('add', 0), ('gate0', 1)]

    def run(item, k):
        name, o = item
        now, nxt, nx2, was = k < NA, k + 1 < NA, k + 2 < NA, 0 <= k - 1 < NA
        if name in ("qkv", "square", "values", "squares", "rotate"):
            if nx2:
                {"qkv": qkv, "square": square, "values": values, "squares": squares, "rotate": rotate}[name](k + 2)
        elif name == "qkT":
            if nxt:
                qkT(k + 1, o)
        elif name == "norms":
            if nxt:
                norms(k + 1)
        elif name in ("scores", "softmax", "exps", "normalise", "eT"):
            if now:
                {"scores": scores, "softmax": softmax, "exps": exps, "normalise": normalise, "eT": eT}[name](k)
        elif name in ("av", "outT", "proj", "add"):
            if was:
                {"av": av, "outT": outT, "proj": proj, "add": add}[name](k - 1)
        elif name == "once":
            if k < 4:
                for stage in range(3):
                    onward(8 + 2 * k, stage)
                if k in (1, 3):
                    xT(2 + k // 2)
            if 8 <= k < 15:
                later(k - 8)
        else:
            q, r = divmod(k - 6, 4)
            if k >= NA or r != o % 4:
                return
            q -= o // 4
            if not 0 <= q < NG:
                return
            if name == "gate0" or name == "gate1" or name == "gate2":
                gate(q, int(name[4]))
            elif name[0:2] == "up":
                up(q, int(name[2]))
            elif name == "turn":
                if q + 4 < NG:
                    xT(q + 4)
                elif q < NG - 3:
                    finish(q)
            elif name == "norm":
                m = F[q]["nrm"]()
                F[q]["nrm"] = lambda: m
            else:
                {"shift": shift, "hT": hT, "gelu": gelu, "down": down}[name](q)

    def last():
        q = NG - 1
        shift(q, 6)
        for c in range(3):
            if "gt%d" % c not in F[q - 1]:
                gate(q - 1, c, c)
        if "ge" not in F[q - 1]:
            gelu(q - 1)
        m = F[q]["nrm"]()
        F[q]["nrm"] = lambda: m
        for c in range(3):
            if "up%d" % c not in F[q - 1]:
                up(q - 1, c, (3, 4, 5)[c])
        hT(q, 7)
        for c in range(3):
            gate(q, c, c)
        gelu(q)
        finish(q - 2)
        down(q - 1, 3)
        for c in range(3):
            up(q, c, 4 + c)
        finish(q - 1)
        down(q, 7)
        finish(q)

    for q in range(2):
        xT(q)
    for f in range(2):
        for s in range(2):
            table(0, f, s)
    for f in (qkv, square, values, squares, rotate):
        f(0)
    for f in (qkv, square, values):
        f(1)
    norms(0)
    qkT(0, 0)
    qkT(0, 1)
    squares(1)
    rotate(1)
    for k in range(NA + 1):
        for item in STEP:
            run(item, k)
    last()
    sp.ops.append((s_out, 16 * 4))


def constants():
    i = np.arange(P)
    causal = np.zeros((2, P, P), np.float32)
    causal[0] = np.where(i[None, :] <= i[:, None], 0.0, -BIG)
    causal[1] = causal[0].T
    c = np.arange(P)[None, :]
    w = i[:, None] % DH
    ok = (c - DH <= w) & (w <= c)
    band = np.stack([ok, ok & ((i[:, None] >= DH) | (c >= DH))])
    band = np.where(band, 0.0, -BIG).astype(np.float32)
    shift = np.zeros((2, P, P), np.float32)
    shift[0, i[:-1], i[1:]] = 1.0
    shift[1, P - 1, 0] = 1.0
    f = np.float32
    hidx = np.arange(0, DH, 2, dtype=f)
    inv = (f(1.0) / np.power(f(10000.0), hidx / f(DH))).astype(f)
    t = np.arange(NT, dtype=f)
    fr = (t[:, None] * inv[None, :]).astype(f)
    fr = np.concatenate([fr, fr], -1).astype(np.float64)
    base = ((hidx + f(0.4 * DH)) / f(1.4 * DH)).astype(f)
    power = ((t - NT // 2) / f(32.0)).astype(f)
    sc = base[None, :].astype(np.float64) ** power[:, None].astype(np.float64)
    sc = np.concatenate([sc, sc], -1)
    sign = np.concatenate([-np.ones(DH // 2), np.ones(DH // 2)])
    cos, sin = np.cos(fr), np.sin(fr) * sign
    rot = np.stack([np.stack([cos * sc, cos / sc], 1), np.stack([sin * sc, sin / sc], 1)]).astype(f)
    return {"c_ident": np.eye(P, dtype=f), "c_causal": causal, "c_band": band, "c_shift": shift, "c_rot": rot}


def kernel(**inputs):
    import concourse.bacc as bacc
    from concourse.bass_utils import run_bass_kernel_spmd

    nc = bacc.Bacc("TRN2", target_bir_lowering=False, num_devices=1)
    arrays = {k: np.ascontiguousarray(v) for k, v in inputs.items()}
    arrays.update(constants())
    I = {k: nc.dram_tensor("in_" + k, a.shape, mybir.dt.from_np(a.dtype), kind="ExternalInput").ap() for k, a in arrays.items()}
    out = nc.dram_tensor("out_0", (NB, NT, DM), F32, kind="ExternalOutput").ap()
    program(nc, I, out)
    r = run_bass_kernel_spmd(nc, [{"in_" + k: a for k, a in arrays.items()}], core_ids=[0])
    return r.results[0]["out_0"]
```
